# Optimizing a Trainium2 kernel written in Bass

```python
import numpy as np
import jax
import jax.numpy as jnp

def _softmax(x, axis=-1):
    return jax.nn.softmax(x, axis=axis)

def _gelu(x):
    return jax.nn.gelu(x, approximate=True)

def _silu(x):
    return jax.nn.silu(x)

def _sigmoid(x):
    return jax.nn.sigmoid(x)

def _layernorm(x, axis=-1, eps=1e-05):
    m = jnp.mean(x, axis=axis, keepdims=True)
    v = jnp.var(x, axis=axis, keepdims=True)
    return (x - m) / jnp.sqrt(v + eps)

def _scatter_add(tgt, idx, src, axis=0):
    return tgt.at[idx].add(src)

def _segment_sum(src, seg, n):
    return jax.ops.segment_sum(src, seg, n)
kernel_name = 'mk_cond_seq_d2_seqx_r4_797be2'

def setup_inputs(seed: int=0):
    np.random.seed(seed)
    _w = jnp.asarray

    def _rec_inputs():
        import jax
        import jax.numpy as jnp
        _rk = jax.random.key(seed)
        x = -0.000125 + 0.9999 * jax.random.normal(jax.random.fold_in(_rk, 1), (8, 256, 256), jnp.float32)
        _lenS = 256 - jax.random.randint(jax.random.fold_in(_rk, 7), (8,), 0, max(1, 256 // 4) + 1, jnp.int32)
        _lenS2 = 256 - jax.random.randint(jax.random.fold_in(_rk, 8), (8,), 0, max(1, 256 // 4) + 1, jnp.int32)
        cond_256 = 0.0061147 + 1.02565 * jax.random.normal(jax.random.fold_in(_rk, 11), (8, 64), jnp.float32)
        fside_BxS_0 = -0.00265932 + 1.00408 * jax.random.normal(jax.random.fold_in(_rk, 12), (8, 256), jnp.float32)
        return (x, cond_256, fside_BxS_0)
    x, cond_256, fside_BxS_0 = _rec_inputs()

    def _L0_cond_setup():
        import jax, jax.numpy as jnp
        import numpy as np
        DIM = 256
        BN = 128
        H = 64
        DELTA_SCALE = 0.1
        key = jax.random.key(seed)
        ks = jax.random.split(key, 10)
        B, L = (16, 512)

        def init(k, shape, fan_in):
            bound = 1.0 / np.sqrt(fan_in)
            return jax.random.uniform(k, shape, jnp.float32, -bound, bound)
        return {'x': jax.random.normal(ks[0], (B, L, DIM), jnp.float32), 'h_lang': jax.random.normal(ks[1], (B, H), jnp.float32), 'Wd': init(ks[2], (BN, DIM), DIM), 'bd': init(ks[3], (BN,), DIM), 'Wu': init(ks[4], (DIM, BN), BN), 'bu': init(ks[5], (DIM,), BN), 'Wdd': init(ks[6], (BN * DIM, H), H), 'bdd': init(ks[7], (BN * DIM,), H), 'Wdu': init(ks[8], (DIM * BN, H), H), 'bdu': init(ks[9], (DIM * BN,), H)}
    _L0_cond_all = _L0_cond_setup()
    _L0_cond_in = {k: v for k, v in _L0_cond_all.items() if k in ('Wd', 'bd', 'Wu', 'bu', 'Wdd', 'bdd', 'Wdu', 'bdu')}
    del _L0_cond_all

    def _L1_cond_setup():
        import jax, jax.numpy as jnp
        import numpy as np
        import math
        H = 256
        NH = 16
        DH = H // NH
        EPS = 1e-05

        def _layernorm(x):
            m = jnp.mean(x, axis=-1, keepdims=True)
            v = jnp.mean((x - m) ** 2, axis=-1, keepdims=True)
            return (x - m) / jnp.sqrt(v + EPS)

        def _gelu_tanh(x):
            c = math.sqrt(2.0 / math.pi)
            return 0.5 * x * (1.0 + jnp.tanh(c * (x + 0.044715 * x ** 3)))
        key = jax.random.key(seed)
        ks = jax.random.split(key, 12)
        B, P = (16, 256)
        s = 0.02
        inp = {'x': jax.random.normal(ks[0], (B, P, H), jnp.float32), 't_embd': jax.random.normal(ks[1], (B, 64), jnp.float32), 'c_embd': jax.random.normal(ks[2], (B, H), jnp.float32), 'W_t1': jax.random.normal(ks[3], (H, 64), jnp.float32) * s, 'b_t1': jnp.zeros((H,), jnp.float32), 'W_t2': jax.random.normal(ks[4], (H, H), jnp.float32) * s, 'b_t2': jnp.zeros((H,), jnp.float32), 'W_c': jax.random.normal(ks[5], (6 * H, H), jnp.float32) * s, 'b_c': jnp.zeros((6 * H,), jnp.float32), 'W_qkv': jax.random.normal(ks[6], (3 * H, H), jnp.float32) * s, 'b_qkv': jnp.zeros((3 * H,), jnp.float32), 'W_o': jax.random.normal(ks[7], (H, H), jnp.float32) * s, 'b_o': jnp.zeros((H,), jnp.float32), 'W_f1': jax.random.normal(ks[8], (4 * H, H), jnp.float32) * s, 'b_f1': jnp.zeros((4 * H,), jnp.float32), 'W_f2': jax.random.normal(ks[9], (H, 4 * H), jnp.float32) * s, 'b_f2': jnp.zeros((H,), jnp.float32)}
        return inp
    _L1_cond_all = _L1_cond_setup()
    _L1_cond_in = {k: v for k, v in _L1_cond_all.items() if k in ('W_t1', 'b_t1', 'W_t2', 'b_t2', 'W_c', 'b_c', 'W_qkv', 'b_qkv', 'W_o', 'b_o', 'W_f1', 'b_f1', 'W_f2', 'b_f2')}
    del _L1_cond_all
    return {'x': x, 'cond_256': cond_256, 'fside_BxS_0': fside_BxS_0, 'L0_cond_Wd': _L0_cond_in['Wd'], 'L0_cond_bd': _L0_cond_in['bd'], 'L0_cond_Wu': _L0_cond_in['Wu'], 'L0_cond_bu': _L0_cond_in['bu'], 'L0_cond_Wdd': _L0_cond_in['Wdd'], 'L0_cond_bdd': _L0_cond_in['bdd'], 'L0_cond_Wdu': _L0_cond_in['Wdu'], 'L0_cond_bdu': _L0_cond_in['bdu'], 'L1_cond_W_t1': _L1_cond_in['W_t1'], 'L1_cond_b_t1': _L1_cond_in['b_t1'], 'L1_cond_W_t2': _L1_cond_in['W_t2'], 'L1_cond_b_t2': _L1_cond_in['b_t2'], 'L1_cond_W_c': _L1_cond_in['W_c'], 'L1_cond_b_c': _L1_cond_in['b_c'], 'L1_cond_W_qkv': _L1_cond_in['W_qkv'], 'L1_cond_b_qkv': _L1_cond_in['b_qkv'], 'L1_cond_W_o': _L1_cond_in['W_o'], 'L1_cond_b_o': _L1_cond_in['b_o'], 'L1_cond_W_f1': _L1_cond_in['W_f1'], 'L1_cond_b_f1': _L1_cond_in['b_f1'], 'L1_cond_W_f2': _L1_cond_in['W_f2'], 'L1_cond_b_f2': _L1_cond_in['b_f2']}

def reference(x, cond_256, fside_BxS_0, L0_cond_Wd, L0_cond_bd, L0_cond_Wu, L0_cond_bu, L0_cond_Wdd, L0_cond_bdd, L0_cond_Wdu, L0_cond_bdu, L1_cond_W_t1, L1_cond_b_t1, L1_cond_W_t2, L1_cond_b_t2, L1_cond_W_c, L1_cond_b_c, L1_cond_W_qkv, L1_cond_b_qkv, L1_cond_W_o, L1_cond_b_o, L1_cond_W_f1, L1_cond_b_f1, L1_cond_W_f2, L1_cond_b_f2):
    import jax
    import jax.numpy as jnp

    def _L0_cond_ref(x, h_lang, Wd, bd, Wu, bu, Wdd, bdd, Wdu, bdu):
        import jax, jax.numpy as jnp
        import numpy as np
        DIM = 256
        BN = 128
        H = 64
        DELTA_SCALE = 0.1
        B, L, D = x.shape
        dWd = ((h_lang @ Wdd.T + bdd) * DELTA_SCALE).reshape(B, BN, D)
        dWu = ((h_lang @ Wdu.T + bdu) * DELTA_SCALE).reshape(B, D, BN)
        Wd_b = Wd + dWd
        Wu_b = Wu + dWu
        down = jax.nn.relu(jnp.einsum('bld,bnd->bln', x, Wd_b) + bd)
        up = jnp.einsum('bln,bdn->bld', down, Wu_b) + bu
        return x + up

    def _L1_cond_ref(x, t_embd, c_embd, W_t1, b_t1, W_t2, b_t2, W_c, b_c, W_qkv, b_qkv, W_o, b_o, W_f1, b_f1, W_f2, b_f2):
        import jax, jax.numpy as jnp
        import numpy as np
        import math
        H = 256
        NH = 16
        DH = H // NH
        EPS = 1e-05

        def _layernorm(x):
            m = jnp.mean(x, axis=-1, keepdims=True)
            v = jnp.mean((x - m) ** 2, axis=-1, keepdims=True)
            return (x - m) / jnp.sqrt(v + EPS)

        def _gelu_tanh(x):
            c = math.sqrt(2.0 / math.pi)
            return 0.5 * x * (1.0 + jnp.tanh(c * (x + 0.044715 * x ** 3)))
        B, P, _ = x.shape
        t = jax.nn.silu(t_embd @ W_t1.T + b_t1) @ W_t2.T + b_t2
        cond = jax.nn.silu(t + c_embd) @ W_c.T + b_c
        g1, b1, g2, b2, a1, a2 = jnp.split(cond, 6, axis=-1)
        res1 = x
        h = _layernorm(x) * g1[:, None, :] + b1[:, None, :]
        qkv = h @ W_qkv.T + b_qkv
        q, k, v = jnp.split(qkv, 3, axis=-1)
        q = q.reshape(B, P, NH, DH).transpose(0, 2, 1, 3)
        k = k.reshape(B, P, NH, DH).transpose(0, 2, 1, 3)
        v = v.reshape(B, P, NH, DH).transpose(0, 2, 1, 3)
        scores = jnp.einsum('bhqd,bhkd->bhqk', q, k) / math.sqrt(DH)
        attn = jax.nn.softmax(scores, axis=-1)
        o = jnp.einsum('bhqk,bhkd->bhqd', attn, v)
        o = o.transpose(0, 2, 1, 3).reshape(B, P, H)
        o = o @ W_o.T + b_o
        x = res1 + o * a1[:, None, :]
        res2 = x
        h = _layernorm(x) * g2[:, None, :] + b2[:, None, :]
        h = _gelu_tanh(h @ W_f1.T + b_f1) @ W_f2.T + b_f2
        x = res2 + h * a2[:, None, :]
        return x
    x = _L0_cond_ref(x, cond_256, L0_cond_Wd, L0_cond_bd, L0_cond_Wu, L0_cond_bu, L0_cond_Wdd, L0_cond_bdd, L0_cond_Wdu, L0_cond_bdu)
    x = _L1_cond_ref(x, cond_256, fside_BxS_0, L1_cond_W_t1, L1_cond_b_t1, L1_cond_W_t2, L1_cond_b_t2, L1_cond_W_c, L1_cond_b_c, L1_cond_W_qkv, L1_cond_b_qkv, L1_cond_W_o, L1_cond_b_o, L1_cond_W_f1, L1_cond_b_f1, L1_cond_W_f2, L1_cond_b_f2)
    return x

_drawn_inputs = setup_inputs


def setup_inputs(seed=0):
    import zlib

    import numpy as np

    out = dict(_drawn_inputs(seed))
    spreads = {'L1_cond_b_t1': (0.0, 0.8),
     'L1_cond_b_t2': (0.0, 0.8),
     'L1_cond_b_c': (0.0, 0.635),
     'L1_cond_b_qkv': (0.0, 0.8),
     'L1_cond_b_o': (0.0, 0.457),
     'L1_cond_b_f1': (0.0, 0.8),
     'L1_cond_b_f2': (0.0, 0.436)}
    factors = {'L0_cond_bd': 3.124,
     'L1_cond_W_t1': 8.0,
     'L1_cond_W_t2': 8.0,
     'L1_cond_W_qkv': 8.0,
     'L1_cond_W_o': 7.736,
     'L1_cond_W_f1': 8.0,
     'L1_cond_W_f2': 7.088}
    for name, (base, spread) in spreads.items():
        noise = np.random.default_rng([zlib.crc32(name.encode()), seed]).standard_normal(out[name].shape)
        drawn = base * np.exp(spread * noise) if base else spread * noise
        out[name] = jnp.asarray(drawn.astype(out[name].dtype))
    for name, factor in factors.items():
        out[name] = (out[name] * factor).astype(out[name].dtype)
    return out
```

```python
import concourse.bass as bass
from concourse import mybir
from contextlib import ExitStack

FP32 = mybir.dt.float32
F32R = mybir.dt.float32r
ALU = mybir.AluOpType
ACT = mybir.ActivationFunctionType
AX = mybir.AxisListType

B = 8
P = 256
D = 256
BN = 128
HC = 64
NH, DH = 16, 16
F = 1024
KT = D // 128
TT = P // 128
FT = F // 128
EPS = 1e-5
DELTA_SCALE = 0.1

G, HALF, PP = 2, 2, 4
SET = G * HALF
STK = 3 * DH
MROW = 2 * STK
K_PARTS = (0, 1, 0)
Q_PARTS = (0, 0, 1)

KH = 2
NCHUNK = 16
CHUNK = 2048
RING = 3

C_BD, C_BT1, C_BT2, C_EMB = 0, 1, 3, 5
C_BC = C_EMB + KT * B
C_BQKV = C_BC + 8 * B
C_BF1 = C_BQKV + 6 * B
C_END = C_BF1 + FT * B

T_G1, T_QB, T_KB, T_VB, T_G2, T_F1 = 0, 2, 4, 6, 8, 10
NPAR = 18
NPAR_A = 6

SM_STEPS = NH // 2 * TT
ST_STEPS = NH // 2


def build(nc, x_tok, x_feat, cols_in, hbd_in, ident_in, base_in, small_w, wc_in, wqkv_in, wf1_in, wdelta_in,
          wf2_in, wo_in, rows_in, bcrow_in, out):
    ctx = ExitStack()
    with ctx:
        def sb(name, shape, dt=FP32):
            return ctx.enter_context(nc.sbuf_tensor(name, shape, dt))

        def sem(name):
            return ctx.enter_context(nc.semaphore(name))

        wqkv = [sb(f"wqkv_{p}", [128, KT, 3 * D], F32R) for p in ("hi", "lo")]
        wo = [sb(f"wo_{p}", [128, KT, D], F32R) for p in ("hi", "lo")]
        wf1 = [sb(f"wf1_{p}", [128, KT, F], F32R) for p in ("hi", "lo")]
        wf2 = [sb(f"wf2_{p}", [128, FT, D], F32R) for p in ("hi", "lo")]
        k_stack = [sb(f"k_stack{i}", [128, PP, G, P], F32R) for i in range(2)]
        q_stack = [sb(f"q_stack{i}", [128, HALF, PP, G, P], F32R) for i in range(2)]
        ring = sb("ring", [128, RING, CHUNK])
        probs = [ring[:, i, :].rearrange("p (j t q) -> p j t q", j=PP, t=TT) for i in range(2)]
        gelu_f = ring[:, 2, :].rearrange("p (f n) -> p f n", f=FT)
        g_hi = sb("g_hi", [128, FT, P], F32R)
        g_lo = sb("g_lo", [128, FT, P], F32R)
        qk_parts = g_hi[:, :, :].rearrange("p (w h g) n -> p w h g n", w=2, h=2)
        arena = sb("arena", [128, 6656])
        wc = arena[:, 0:3072].rearrange("p (k n) -> p k n", k=KT)
        wqkv_f = arena[:, 3072:4608].rearrange("p (k n) -> p k n", k=KT)
        wf1_f = arena[:, 4608:6656].rearrange("p (k n) -> p k n", k=KT)
        wt1 = arena[0:HC, 4608:4864]
        wt2 = arena[:, 4864:5376].rearrange("p (k n) -> p k n", k=KT)
        cond_t = arena[0:HC, 5376:5376 + B]

        def tile(at):
            return arena[:, at:at + 512].rearrange("p (t n) -> p t n", t=2)
        x_in = tile(0)
        x1 = [tile(512), tile(1024)]
        x2 = tile(1536)
        xT = tile(2048)
        h1 = tile(2560)
        h2 = tile(3072)
        o_tok = tile(3584)
        a12 = tile(4096)
        v_aug = [arena[:, 4608 + i * 1024:5632 + i * 1024].rearrange("p (t h n) -> p t h n", t=TT, h=NH)
                 for i in range(2)]
        o_aug = sb("o_aug", [128, SET, P])
        dtmp = o_aug[:, :, :].rearrange("p (i s) n -> p i (s n)", i=2)
        w_ad = sb("w_ad", [128, B, 2 * D])
        base = sb("base", [128, 1024])
        downT = base[:, 0:256]
        wd_cur = base[:, 256:512].rearrange("p (k n) -> p k n", k=KT)
        a1bo = base[:, 512:768]
        a2bf2 = base[:, 768:1024]
        h1T = [sb(f"h1T_{p}", [128, KT, P], F32R) for p in ("hi", "lo")]
        h2T = [sb(f"h2T_{p}", [128, KT, P], F32R) for p in ("hi", "lo")]
        oT = [sb(f"oT_{p}", [128, KT, P], F32R) for p in ("hi", "lo")]
        ident = sb("ident", [128, 128])
        hbd = sb("hbd", [128, KH, 32])
        cols = sb("cols", [128, C_END])
        rows = sb("rows", [128, 3, D])
        par = sb("par", [128, B, NPAR])
        par_a = sb("par_a", [128, NPAR_A])
        par_t = sb("par_t", [128, NPAR - NPAR_A])
        s1 = sb("s1", [128, KT, B])
        z2 = sb("z2", [128, KT, B])
        s2 = sb("s2", [128, KT, B])
        mod = sb("mod", [128, 8, B])
        negmax = sb("negmax", [128, TT, NH])
        negmaxT = sb("negmaxT", [NH, P], F32R)
        rden = sb("rden", [128, TT, NH])
        neghalf = sb("neghalf", [128, TT])
        eps = sb("eps", [128, TT])
        bn1 = sb("bn1", [128, TT, 6])
        bn2 = sb("bn2", [128, TT, 6])
        mv1 = sb("mv1", [128, TT, 2])
        mv2 = sb("mv2", [128, TT, 2])
        ve1 = sb("ve1", [128, TT])
        ve2 = sb("ve2", [128, TT])
        rs1 = sb("rs1", [128, TT])
        rs2 = sb("rs2", [128, TT])
        a_sb = sb("a_sb", [B, 2 * D])

        SX = ctx.enter_context(nc.psum_tensor("SX", [128, 4, 512], FP32))
        PV = ctx.enter_context(nc.psum_tensor("PV", [128, 2, 512], FP32))
        MM = ctx.enter_context(nc.psum_tensor("MM", [128, 2, 512], FP32))

        qk_scr = nc.dram_tensor("qk_scr", (2, 128, 2, G * P), FP32).ap()
        a_scr = nc.dram_tensor("a_scr", (B, 2 * D), FP32).ap()

        (ld_const, ld_small, ld_wc, ld_wqkv, ld_wf1, ld_x, ld_xT, ld_a12, stored, a_saved) = map(sem, (
            "ld_const", "ld_small", "ld_wc", "ld_wqkv", "ld_wf1", "ld_x", "ld_xT", "ld_a12", "stored", "a_saved"))
        ld_ring = [sem(f"ld_ring{i}") for i in range(RING)]
        (delta_done, delta_copied, deltaT_done, delta_ready) = map(sem, (
            "delta_done", "delta_copied", "deltaT_done", "delta_ready"))
        (pe_cond, act_cond, dve_cond, w_hi, w_lo, init_done, pool_init, ones_set) = map(sem, (
            "pe_cond", "act_cond", "dve_cond", "w_hi", "w_lo", "init_done", "pool_init",
            "ones_set"))
        (xb_ready, wd_ready, pa_ready, pt_ready, down_done, relu_ready, up_done, x1_ready, st1_ready, rs1_ready,
         h1_ready, h1tr_done, h1T_hi, h1T_lo, q_done, q_hi, q_lo, k_done, k_hi, k_lo, v_done, v_ready) = map(sem, (
            "xb_ready", "wd_ready", "pa_ready", "pt_ready", "down_done", "relu_ready", "up_done", "x1_ready",
            "st1_ready", "rs1_ready", "h1_ready", "h1tr_done", "h1T_hi", "h1T_lo", "q_done", "q_hi", "q_lo",
            "k_done", "k_hi", "k_lo", "v_done", "v_ready"))
        (q_saved, k_saved, q_stacked, k_stacked, sm_done, sm_read, mtr_done, negmaxT_ready, m_stacked, st_done,
         exp_done, pv_done, o_copied, otr_done, rden_ready, o_ready, ontr_done, oT_hi, oT_lo, wo_done) = map(sem, (
            "q_saved", "k_saved", "q_stacked", "k_stacked", "sm_done", "sm_read", "mtr_done", "negmaxT_ready",
            "m_stacked", "st_done", "exp_done", "pv_done", "o_copied", "otr_done", "rden_ready", "o_ready",
            "ontr_done", "oT_hi", "oT_lo", "wo_done"))
        (a1bo_ready, x2base_ready, a1o_ready, x2_ready, st2_ready, rs2_ready, h2_ready, x2b_ready, h2tr_done, h2T_hi,
         h2T_lo, f1_done, gelu_done, g_hi_done, g_lo_done, f2_done, a2y_ready, x3_ready, ve1_ready, ve2_ready,
         bns1_ready, bns2_ready) = map(sem, (
            "a1bo_ready", "x2base_ready", "a1o_ready", "x2_ready", "st2_ready", "rs2_ready", "h2_ready", "x2b_ready",
            "h2tr_done", "h2T_hi", "h2T_lo", "f1_done", "gelu_done", "g_hi_done", "g_lo_done", "f2_done",
            "a2y_ready", "x3_ready", "ve1_ready", "ve2_ready",
            "bns1_ready", "bns2_ready"))

        def nth(b, n, k):
            return b * n + k

        def one(b):
            return b.unsqueeze(1).to_broadcast([128, TT, D])

        block = ctx.enter_context(nc.Block())

        @block.sync
        def _(sp):
            def load_chunk(n):
                if n >= RING:
                    if n - RING < NCHUNK:
                        sp.wait_ge(delta_done, n - RING + 1)
                src = wdelta_in[n] if n < NCHUNK else (wf2_in if n == NCHUNK else wo_in)
                sp.dma_start(ring[:, n % RING, 0:src.shape[1]], src).then_inc(ld_ring[n % RING], 16)

            def load_front(b):
                sp.dma_start(xT, x_feat[bass.ds(b, 1)].rearrange("o (k p) n -> p (o k) n", p=128)).then_inc(ld_xT, 16)
                sp.dma_start(x_in, x_tok[bass.ds(b, 1)].rearrange("o (t p) n -> p (o t) n", p=128)).then_inc(ld_x, 16)

            def load_a12(b):
                sp.dma_start(a12.rearrange("p t n -> p (t n)"),
                             a_scr[bass.ds(b, 1), :].to_broadcast([128, 2 * D])).then_inc(ld_a12, 16)

            def stack(b, par_):
                for w, hi, lo, saved in ((0, q_hi, q_lo, q_saved), (1, k_hi, k_lo, k_saved)):
                    sp.wait_ge(hi, nth(b, 1, 1))
                    sp.wait_ge(lo, nth(b, 1, 1))
                    sp.dma_start(qk_scr[w], qk_parts[:, w].rearrange("p h g n -> p h (g n)").bitcast(FP32))\
                      .then_inc(saved, 16)
                for w, parts, saved, done in ((0, Q_PARTS, q_saved, q_stacked), (1, K_PARTS, k_saved, k_stacked)):
                    sp.wait_ge(saved, nth(b, 16, 16))
                    for half in range(HALF):
                        for slot, part in enumerate(parts):
                            at = half * STK + slot * DH
                            if w == 0:
                                dst = q_stack[par_][at:at + DH, half]
                            else:
                                dst = k_stack[par_][at:at + DH]
                            src = qk_scr[w, half * 64:half * 64 + 64, part].rearrange("(j d) n -> d j n", d=DH)
                            sp.dma_start(dst.rearrange("d j g n -> d j (g n)").bitcast(FP32), src).then_inc(done, 16)

            def phase1(i, par_, front, tail):
                sp.wait_ge(negmaxT_ready, nth(i, 1, 1))
                sp.dma_start(q_stack[par_][MROW:MROW + 1].rearrange("o a j g n -> o (a j g) n").bitcast(FP32),
                             negmaxT[:, :].bitcast(FP32)).then_inc(m_stacked, 16)
                if front:
                    stack(i + 1, 1 - par_)
                if tail:
                    sp.wait_ge(x3_ready, nth(i - 1, 1, 1))
                    sp.dma_start(out[bass.ds(i - 1, 1)].rearrange("o (t p) n -> p (o t) n", p=128), x2)\
                      .then_inc(stored, 16)
                load_a12(i)

            sp.dma_start(cols[:, :], cols_in).then_inc(ld_const, 16)
            sp.dma_start(hbd[:, :, :], hbd_in).then_inc(ld_const, 16)
            sp.dma_start(arena[:, 4608:5376 + B], small_w).then_inc(ld_small, 16)
            load_chunk(0)
            sp.dma_start(base[:, :], base_in).then_inc(ld_const, 16)
            sp.dma_start(ident[:, :], ident_in).then_inc(ld_const, 16)
            load_chunk(1)
            sp.dma_start(wc, wc_in).then_inc(ld_wc, 16)
            sp.dma_start(a_sb[:, :], bcrow_in).then_inc(ld_wc, 16)
            load_chunk(2)
            sp.dma_start(wqkv_f, wqkv_in).then_inc(ld_wqkv, 16)
            load_chunk(3)
            sp.wait_ge(pe_cond, 2)
            sp.dma_start(wf1_f, wf1_in).then_inc(ld_wf1, 16)
            for n in range(4, NCHUNK):
                load_chunk(n)
            sp.dma_start(rows[:, :, :], rows_in).then_inc(ld_const, 16)
            sp.wait_ge(pe_cond, 4)
            load_front(0)
            load_chunk(NCHUNK)
            load_chunk(NCHUNK + 1)
            sp.wait_ge(dve_cond, 3)
            sp.dma_start(a_scr, a_sb[:, :]).then_inc(a_saved, 16)
            stack(0, 0)
            sp.wait_ge(down_done, 1)
            sp.wait_ge(x1_ready, 1)
            load_front(1)
            sp.wait_ge(a_saved, 16)
            phase1(0, 0, True, False)

            def loads_ahead(i):
                sp.wait_ge(down_done, nth(i, 1, 1))
                sp.wait_ge(x1_ready, nth(i, 1, 1))
                load_front(i + 1)
            with sp.Fori(1, B - 2, 2) as i0:
                for u in range(2):
                    i = i0 + u
                    loads_ahead(i)
                    phase1(i, (1 + u) % 2, True, True)
            phase1(B - 1, 1, False, True)
            sp.wait_ge(x3_ready, B)
            sp.dma_start(out[B - 1].rearrange("(t p) n -> p t n", p=128), x2).then_inc(stored, 16)
            sp.wait_ge(stored, 16 * B)

        @block.gpsimd
        def _(pool):
            def rstd(b, st_ready, mv, ve, ve_ready, rs, rs_ready):
                pool.wait_ge(st_ready, nth(b, 1, 1))
                pool.tensor_tensor(ve[:, :], mv[:, :, 1], eps[:, :], ALU.add).then_inc(ve_ready, 1)
                pool.wait_ge(ve_ready, nth(b, 1, 1))
                pool.tensor_tensor(rs[:, :], ve[:, :], neghalf[:, :], ALU.pow).then_inc(rs_ready, 1)

            def front(b):
                pool.wait_ge(ld_x, nth(b, 16, 16))
                pool.tensor_tensor(x_in, x_in, one(rows[:, 0, :]), ALU.add).then_inc(xb_ready, 1)
                rstd(b, st1_ready, mv1, ve1, ve1_ready, rs1, rs1_ready)

            def before_tail(b, par_, first=False):
                pool.wait_ge(ld_a12, nth(b, 16, 16))
                if not first:
                    pool.wait_ge(stored, nth(b, 16, 0))
                    pool.wait_ge(x3_ready, nth(b, 1, 0))
                pool.tensor_tensor(a1bo, a12[:, 0, :], rows[:, 1, :], ALU.mult).then_inc(a1bo_ready, 1)
                pool.tensor_tensor(a2bf2, a12[:, 1, :], rows[:, 2, :], ALU.mult).then_inc(a1bo_ready, 1)
                pool.wait_ge(a1bo_ready, nth(b, 2, 1))
                pool.wait_ge(x1_ready, nth(b, 1, 1))
                pool.tensor_tensor(x2, x1[par_], one(a1bo), ALU.add).then_inc(x2base_ready, 1)

            def tail(b):
                rstd(b, st2_ready, mv2, ve2, ve2_ready, rs2, rs2_ready)
                pool.wait_ge(h2_ready, nth(b, 1, 1))
                pool.wait_ge(a1bo_ready, nth(b, 2, 2))
                pool.tensor_tensor(x2, x2, one(a2bf2), ALU.add).then_inc(x2b_ready, 1)

            pool.memset(neghalf[:, :], -0.5).then_inc(pool_init, 1)
            pool.memset(eps[:, :], EPS).then_inc(pool_init, 1)
            for i in range(2):
                pool.memset(q_stack[i][:, :, :, :, :].bitcast(FP32), 0.0).then_inc(pool_init, 1)
            pool.wait_ge(ld_const, 16 * 5)
            pool.wait_ge(pool_init, 4)
            front(0)
            front(1)
            before_tail(0, 0, first=True)
            with pool.Fori(1, B - 2, 2) as i0:
                for u in range(2):
                    i = i0 + u
                    front(i + 1)
                    tail(i - 1)
                    before_tail(i, (1 + u) % 2)
            tail(B - 2)
            before_tail(B - 1, 1)
            tail(B - 1)

        @block.scalar
        def _(act):
            def front(b, par_, negmax_of=None, tail_of=None):
                if negmax_of is not None:
                    act.wait_ge(mtr_done, nth(negmax_of, 1, 1))
                    act.activation(negmaxT[:, :], SX[0:NH, 3, 0:P], ACT.Copy).then_inc(negmaxT_ready, 1)
                if b is not None:
                    act.wait_ge(down_done, nth(b, 1, 1))
                    act.activation(downT, MM[:, 0, 0:P], ACT.Relu, bias=cols[:, C_BD:C_BD + 1])\
                       .then_inc(relu_ready, 1)
                if tail_of is not None:
                    act.wait_ge(ontr_done, nth(tail_of, 1, 1))
                    act.wait_ge(pt_ready, nth(tail_of, 1, 1))
                    for f in range(KT):
                        last = act.activation(oT[0][:, f, :], SX[:, 2, f * P:(f + 1) * P], ACT.Identity,
                                              bias=par_t[:, f:f + 1])
                    last.then_inc(oT_hi, 1)
                if b is not None:
                    act.wait_ge(h1tr_done, nth(b, 1, 1))
                    act.wait_ge(pa_ready, nth(b, 1, 1))
                    for f in range(KT):
                        last = act.activation(h1T[0][:, f, :], MM[:, 0, f * P:(f + 1) * P], ACT.Copy,
                                              scale=par_a[:, T_G1 + f:T_G1 + f + 1])
                    last.then_inc(h1T_hi, 1)
                    for w, done, hi, bank, col in ((0, q_done, q_hi, 0, T_QB), (1, k_done, k_hi, 1, T_KB)):
                        act.wait_ge(done, nth(b, 1, 1))
                        for g in range(G):
                            last = act.activation(qk_parts[:, w, 0, g, :], SX[:, bank, g * P:(g + 1) * P],
                                                  ACT.Identity, bias=par_a[:, col + g:col + g + 1])
                        last.then_inc(hi, 1)
                if tail_of is not None:
                    act.wait_ge(h2tr_done, nth(tail_of, 1, 1))
                    for f in range(KT):
                        last = act.activation(h2T[0][:, f, :], MM[:, 1, f * P:(f + 1) * P], ACT.Copy,
                                              scale=par_t[:, T_G2 - NPAR_A + f:T_G2 - NPAR_A + f + 1])
                    last.then_inc(h2T_hi, 1)
                if b is not None:
                    act.wait_ge(v_done, nth(b, 1, 1))
                    for t in range(TT):
                        last = act.activation(v_aug[par_][:, t, :, 0:DH],
                                              SX[:, 3, t * D:(t + 1) * D].rearrange("p (h n) -> p h n", n=DH), ACT.Copy)
                    last.then_inc(v_ready, 1)
                if tail_of is not None:
                    for m, bank in enumerate((SX[:, 2], MM[:, 0], MM[:, 1], SX[:, 0])):
                        act.wait_ge(f1_done, nth(tail_of, 4, m + 1))
                        for f in range(2):
                            col = T_F1 - NPAR_A + 2 * m + f
                            last = act.activation(gelu_f[:, 2 * m + f, :], bank[:, f * P:(f + 1) * P],
                                                  ACT.Gelu_apprx_tanh, bias=par_t[:, col:col + 1])
                        last.then_inc(gelu_done, 1)

            def softmax(b):
                for u in range(ST_STEPS):
                    s = u // 2
                    act.wait_ge(st_done, nth(b, ST_STEPS, u + 1))
                    if s >= 2 and u % 2 == 0:
                        act.wait_ge(pv_done, nth(b, SET, s - 1))
                    j = 2 * (u % 2)
                    act.activation(probs[s % 2][:, j:j + 2].rearrange("p j t q -> p (j t q)"),
                                   SX[:, j:j + 2, :].rearrange("p a n -> p (a n)"), ACT.Exp, scale=DH ** -0.5)\
                       .then_inc(exp_done, 1)
                    if u == 6:
                        act.wait_ge(pv_done, nth(b, SET, 2))
                        act.activation(o_aug[:, 0:2, :].rearrange("p s n -> p (s n)"), PV[:, 0, :], ACT.Copy)\
                           .then_inc(o_copied, 1)
                act.wait_ge(pv_done, nth(b, SET, 4))
                act.activation(o_aug[:, 2:4, :].rearrange("p s n -> p (s n)"), PV[:, 1, :], ACT.Copy)\
                   .then_inc(o_copied, 1)

            def copy_delta(n):
                act.wait_ge(delta_done, 2 * n + 2)
                if n >= 2:
                    act.wait_ge(deltaT_done, n - 1)
                act.activation(dtmp[:, n % 2, :], SX[:, n % 2, :], ACT.Copy).then_inc(delta_copied, 1)

            act.wait_ge(ld_const, 16 * 4)
            act.wait_ge(pe_cond, 1)
            for f in range(KT):
                last = act.activation(s1[:, f, :], MM[:, 0, f * B:(f + 1) * B], ACT.Silu,
                                      bias=cols[:, C_BT1 + f:C_BT1 + f + 1])
            last.then_inc(act_cond, 1)
            act.wait_ge(dve_cond, 1)
            act.activation(s2[:, :, :], z2[:, :, :], ACT.Silu).then_inc(act_cond, 1)
            copy_delta(0)
            copy_delta(1)
            act.wait_ge(ld_wqkv, 16)
            act.activation(wqkv[0][:, :, :], wqkv_f, ACT.Copy).then_inc(w_hi, 1)
            copy_delta(2)
            act.wait_ge(ld_wf1, 16)
            act.activation(wf1[0][:, :, :], wf1_f, ACT.Copy).then_inc(w_hi, 1)
            for n in range(3, NCHUNK // 2):
                copy_delta(n)
            front(0, 0)
            for n, (w, w_) in enumerate(((NCHUNK, wf2), (NCHUNK + 1, wo))):
                act.wait_ge(ld_ring[w % RING], 16 * (w // RING + 1))
                size = w_[0].shape[1] * D
                act.activation(w_[0][:, :, :].rearrange("p k n -> p (k n)"), ring[:, w % RING, 0:size], ACT.Copy)\
                   .then_inc(w_hi, 1)
            act.wait_ge(w_lo, 4)
            front(1, 1, negmax_of=0)
            softmax(0)
            with act.Fori(1, B - 2, 2) as i0:
                for u in range(2):
                    i = i0 + u
                    front(i + 1, u % 2, negmax_of=i, tail_of=i - 1)
                    softmax(i)
            front(None, 0, negmax_of=B - 1, tail_of=B - 2)
            softmax(B - 1)
            front(None, 0, tail_of=B - 1)

        @block.vector
        def _(dve):
            def cut(lo, x, hi):
                return dve.tensor_tensor(lo, x, hi.bitcast(FP32), ALU.subtract)

            def stats(b, x, ready, bn, bn_ready, mv, st_ready):
                dve.wait_ge(ready, nth(b, 1, 1))
                for t in range(TT):
                    last = dve.bn_stats(bn[:, t, :], x[:, t, :])
                last.then_inc(bn_ready, 1)
                dve.wait_ge(init_done, 1)
                dve.wait_ge(bn_ready, nth(b, 1, 1))
                for t in range(TT):
                    last = dve.bn_aggr(mv[:, t, :], bn[:, t, :])
                last.then_inc(st_ready, 1)

            def normalise(b, h, x, mv, rs, rs_ready, h_ready):
                dve.wait_ge(rs_ready, nth(b, 1, 1))
                for t in range(TT):
                    last = dve.tensor_scalar(h[:, t, :], x[:, t, :], mv[:, t, 0:1], rs[:, t:t + 1],
                                             ALU.subtract, ALU.mult)
                last.then_inc(h_ready, 1)

            def low_part(b, hi_ready, lo_ready, tiles, op):
                dve.wait_ge(hi_ready, nth(b, 1, 1))
                for lo, psum, col, hi in tiles:
                    last = dve.scalar_tensor_tensor(lo, psum, col, hi.bitcast(FP32), op, ALU.subtract)
                last.then_inc(lo_ready, 1)

            def phase1(b, par_, tail_of=None, first=False):
                if b is not None:
                    if not first:
                        dve.wait_ge(down_done, nth(b, 1, 0))
                    dve.tensor_copy(wd_cur, w_ad[:, bass.ds(b, 1), 0:D].rearrange("p o (k n) -> p (o k) n", k=KT))\
                       .then_inc(wd_ready, 1)
                    if not first:
                        dve.wait_ge(k_hi, nth(b, 1, 0))
                        dve.wait_ge(k_lo, nth(b, 1, 0))
                    dve.tensor_copy(par_a[:, :], par[:, bass.ds(b, 1), 0:NPAR_A].rearrange("p o n -> p (o n)"))\
                       .then_inc(pa_ready, 1)
                if tail_of is not None:
                    a = tail_of
                    if not (isinstance(a, int) and a == 0):
                        dve.wait_ge(gelu_done, nth(a, 4, 0))
                    dve.tensor_copy(par_t[:, :], par[:, bass.ds(a, 1), NPAR_A:NPAR].rearrange("p o n -> p (o n)"))\
                       .then_inc(pt_ready, 1)
                    dve.wait_ge(otr_done, nth(a, 1, 1))
                    o4 = SX[:, 0:2, :].rearrange("p t (h n) -> p t h n", n=32)
                    dve.reciprocal(rden[:, :, :], o4[:, :, :, DH]).then_inc(rden_ready, 1)
                    dve.wait_ge(rden_ready, nth(a, 1, 1))
                    for t in range(TT):
                        last = dve.tensor_tensor(o_tok[:, t, :].rearrange("p (h n) -> p h n", n=DH), o4[:, t, :, 0:DH],
                                                 rden[:, t, :].unsqueeze(2).to_broadcast([128, NH, DH]), ALU.mult)
                    last.then_inc(o_ready, 1)
                if b is not None:
                    dve.wait_ge(up_done, nth(b, 1, 1))
                    dve.wait_ge(xb_ready, nth(b, 1, 1))
                    if tail_of is not None:
                        dve.wait_ge(x2base_ready, nth(tail_of, 1, 1))
                    dve.tensor_tensor(x1[par_], MM[:, 1, :].rearrange("p (t n) -> p t n", t=TT), x_in, ALU.add)\
                       .then_inc(x1_ready, 1)
                    stats(b, x1[par_], x1_ready, bn1, bns1_ready, mv1, st1_ready)
                if tail_of is not None:
                    low_part(a, oT_hi, oT_lo, [(oT[1][:, f, :], SX[:, 2, f * P:(f + 1) * P], par_t[:, f:f + 1],
                                                oT[0][:, f, :]) for f in range(KT)], ALU.add)
                if b is not None:
                    normalise(b, h1, x1[par_], mv1, rs1, rs1_ready, h1_ready)
                if tail_of is not None:
                    dve.wait_ge(wo_done, nth(a, 1, 1))
                    dve.wait_ge(x2base_ready, nth(a, 1, 1))
                    dve.tensor_tensor(h2, PV[:, 1, :].rearrange("p (t n) -> p t n", t=TT), one(a12[:, 0, :]), ALU.mult)\
                       .then_inc(a1o_ready, 1)
                    dve.wait_ge(a1o_ready, nth(a, 1, 1))
                    dve.tensor_tensor(x2, x2, h2, ALU.add).then_inc(x2_ready, 1)
                    stats(a, x2, x2_ready, bn2, bns2_ready, mv2, st2_ready)
                if b is not None:
                    low_part(b, h1T_hi, h1T_lo, [(h1T[1][:, f, :], MM[:, 0, f * P:(f + 1) * P],
                                                  par_a[:, T_G1 + f:T_G1 + f + 1], h1T[0][:, f, :])
                                                 for f in range(KT)], ALU.mult)
                if tail_of is not None:
                    normalise(a, h2, x2, mv2, rs2, rs2_ready, h2_ready)
                if b is not None:
                    for w, hi, lo, bank, col in ((0, q_hi, q_lo, 0, T_QB), (1, k_hi, k_lo, 1, T_KB)):
                        low_part(b, hi, lo, [(qk_parts[:, w, 1, g, :], SX[:, bank, g * P:(g + 1) * P],
                                              par_a[:, col + g:col + g + 1], qk_parts[:, w, 0, g, :])
                                             for g in range(G)], ALU.add)
                if tail_of is not None:
                    low_part(a, h2T_hi, h2T_lo, [(h2T[1][:, f, :], MM[:, 1, f * P:(f + 1) * P],
                                                  par_t[:, T_G2 - NPAR_A + f:T_G2 - NPAR_A + f + 1], h2T[0][:, f, :])
                                                 for f in range(KT)], ALU.mult)
                    if b is not None:
                        dve.wait_ge(q_saved, nth(b, 16, 16))
                        dve.wait_ge(k_saved, nth(b, 16, 16))
                    for m in range(4):
                        dve.wait_ge(gelu_done, nth(a, 4, m + 1))
                        two = slice(2 * m, 2 * m + 2)
                        dve.tensor_copy(g_hi[:, two, :], gelu_f[:, two, :]).then_inc(g_hi_done, 1)
                        dve.wait_ge(g_hi_done, nth(a, 4, m + 1))
                        cut(g_lo[:, two, :], gelu_f[:, two, :], g_hi[:, two, :]).then_inc(g_lo_done, 1)
                    dve.wait_ge(f2_done, nth(a, 1, 1))
                    dve.tensor_tensor(h2, PV[:, 0, :].rearrange("p (t n) -> p t n", t=TT), one(a12[:, 1, :]), ALU.mult)\
                       .then_inc(a2y_ready, 1)
                    dve.wait_ge(a2y_ready, nth(a, 1, 1))
                    dve.wait_ge(x2b_ready, nth(a, 1, 1))
                    dve.tensor_tensor(x2, x2, h2, ALU.add).then_inc(x3_ready, 1)

            def row_max(b):
                for n in range(SM_STEPS):
                    s, t, j = n // 4, n // 2 % 2, 2 * (n % 2)
                    g, half = s // HALF, s % HALF
                    at = half * PP * G + j * G + g
                    dve.wait_ge(sm_done, nth(b, SM_STEPS, n + 1))
                    dve.tensor_reduce(negmax[:, t, at:at + G + 1:G], MM[:, n % 2, :].rearrange("p (j n) -> p j n", j=2),
                                      AX.X, ALU.max, negate=True).then_inc(sm_read, 1)

            for i in range(2):
                dve.memset(k_stack[i][MROW:MROW + 1].bitcast(FP32), 1.0).then_inc(ones_set, 1)
            dve.wait_ge(ld_const, 16 * 4)
            dve.wait_ge(pe_cond, 2)
            for f in range(KT):
                last = dve.scalar_tensor_tensor(z2[:, f, :], MM[:, 1, f * B:(f + 1) * B], cols[:, C_BT2 + f:C_BT2 + f + 1],
                                                cols[:, C_EMB + f * B:C_EMB + (f + 1) * B], ALU.add, ALU.add)
            last.then_inc(dve_cond, 1)

            def add_delta(n):
                w = n // 4
                if n == 0:
                    dve.scalar_tensor_tensor(base[:, 0:512], base[:, 512:1024], DELTA_SCALE, base[:, 0:512],
                                             ALU.mult, ALU.add).then_inc(init_done, 1)
                    dve.wait_ge(init_done, 1)
                dve.wait_ge(deltaT_done, n + 1)
                c0 = n * 64
                dve.scalar_tensor_tensor(w_ad[:, :, c0:c0 + 64].rearrange("p b c -> p c b"),
                                         SX[:, 2 + n % 2, :].rearrange("p (c b) -> p c b", b=B), DELTA_SCALE,
                                         base[:, c0:c0 + 64].unsqueeze(2).to_broadcast([128, 64, B]),
                                         ALU.mult, ALU.add).then_inc(delta_ready, 1)

            add_delta(0)
            dve.wait_ge(pe_cond, 3)
            dve.tensor_tensor(mod[:, :, :], MM[:, 0, 0:8 * B].rearrange("p (c b) -> p c b", b=B),
                              cols[:, C_BC:C_BC + 8 * B].rearrange("p (c b) -> p c b", b=B), ALU.add).then_inc(dve_cond, 1)
            dve.wait_ge(pe_cond, 4)
            dve.wait_ge(ld_wc, 32)
            dve.tensor_tensor(a_sb[:, :], MM[0:B, 1, :], a_sb[:, :], ALU.add).then_inc(dve_cond, 1)
            add_delta(1)
            dve.wait_ge(w_hi, 1)
            cut(wqkv[1][:, :, :], wqkv_f, wqkv[0][:, :, :]).then_inc(w_lo, 1)
            dve.wait_ge(dve_cond, 2)
            dve.tensor_copy(par[:, :, T_G1:T_G1 + 2].rearrange("p b c -> p c b"), mod[:, 0:2, :])
            dve.tensor_copy(par[:, :, T_G2:T_G2 + 2].rearrange("p b c -> p c b"), mod[:, 4:6, :])
            dve.wait_ge(pe_cond, 5)
            dve.tensor_tensor(par[:, :, T_QB:T_QB + 6].rearrange("p b c -> p c b"),
                              MM[:, 0, 0:6 * B].rearrange("p (c b) -> p c b", b=B),
                              cols[:, C_BQKV:C_BQKV + 6 * B].rearrange("p (c b) -> p c b", b=B), ALU.add).then_inc(dve_cond, 1)
            add_delta(2)
            dve.wait_ge(w_hi, 2)
            cut(wf1[1][:, :, :], wf1_f, wf1[0][:, :, :]).then_inc(w_lo, 1)
            dve.wait_ge(pe_cond, 6)
            dve.tensor_tensor(par[:, :, T_F1:T_F1 + FT].rearrange("p b c -> p c b"),
                              MM[:, 1, 0:FT * B].rearrange("p (c b) -> p c b", b=B),
                              cols[:, C_BF1:C_BF1 + FT * B].rearrange("p (c b) -> p c b", b=B), ALU.add).then_inc(dve_cond, 1)
            dve.wait_ge(w_lo, 2)
            for i in range(2):
                last = dve.memset(v_aug[i][:, :, :, DH:32], 1.0)
            last.then_inc(init_done, 1)
            for n in range(3, NCHUNK // 2):
                add_delta(n)
            dve.wait_ge(delta_ready, NCHUNK // 2)
            dve.wait_ge(dve_cond, 5)
            phase1(0, 0, first=True)
            for n, w in enumerate((wf2, wo)):
                dve.wait_ge(w_hi, 3 + n)
                c = NCHUNK + n
                size = w[0].shape[1] * D
                cut(w[1][:, :, :].rearrange("p k n -> p (k n)"), ring[:, c % RING, 0:size],
                    w[0][:, :, :].rearrange("p k n -> p (k n)")).then_inc(w_lo, 1)
            row_max(0)
            phase1(1, 1)
            row_max(1)
            with dve.Fori(1, B - 2, 2) as i0:
                for u in range(2):
                    i = i0 + u
                    phase1(i + 1, u % 2, tail_of=i - 1)
                    row_max(i + 1)
            phase1(None, 0, tail_of=B - 2)
            phase1(None, 0, tail_of=B - 1)

        @block.tensor
        def _(pe):
            def three(out, terms, first=True, last=True, **kw):
                n = len(terms)
                for i, (lhs, rhs) in enumerate(terms):
                    for a, c in ((0, 0), (0, 1), (1, 0)):
                        m = pe.matmul(out, lhs[a], rhs[c], start=first and i == 0 and a == c == 0,
                                      stop=last and i == n - 1 and a == 1, **kw)
                return m

            def pair(x, *at):
                return [p[at] for p in x]

            full = slice(None)

            def down(b):
                pe.wait_ge(ld_xT, nth(b, 16, 16))
                pe.wait_ge(wd_ready, nth(b, 1, 1))
                for k in range(KT):
                    m = pe.matmul(MM[:, 0, 0:P], wd_cur[:, k, :], xT[:, k, :], start=k == 0, stop=k == KT - 1)
                m.then_inc(down_done, 1)

            def up(b):
                pe.wait_ge(relu_ready, nth(b, 1, 1))
                for t in range(TT):
                    m = pe.matmul(MM[:, 1, t * D:(t + 1) * D], downT[:, t * 128:(t + 1) * 128],
                                  w_ad[:, bass.ds(b, 1), D:2 * D].rearrange("p o n -> p (o n)"), start=True, stop=True)
                m.then_inc(up_done, 1)

            def transpose4(out, x):
                for f in range(KT):
                    for t in range(TT):
                        m = pe.transpose(out[:, f * P + t * 128:f * P + (t + 1) * 128], x[:, t, f * 128:(f + 1) * 128],
                                         ident[:, :])
                return m

            def h1_transpose(b):
                pe.wait_ge(h1_ready, nth(b, 1, 1))
                transpose4(MM[:, 0, :], h1).then_inc(h1tr_done, 1)

            def project_qk(b, w, done):
                for g in range(G):
                    c = slice((w * G + g) * 128, (w * G + g + 1) * 128)
                    m = three(SX[:, w, g * P:(g + 1) * P],
                              [(pair(wqkv, full, k, c), pair(h1T, full, k, full)) for k in range(KT)])
                m.then_inc(done, 1)

            def project_v(b):
                for t in range(TT):
                    c = slice(t * 128, (t + 1) * 128)
                    m = three(SX[:, 3, t * D:(t + 1) * D],
                              [(pair(h1T, full, k, c), pair(wqkv, full, k, slice(2 * D, 3 * D))) for k in range(KT)])
                m.then_inc(v_done, 1)

            def phase1(b, par_, negmax_of=None, tail_of=None):
                a = tail_of
                if a is not None:
                    pe.wait_ge(exp_done, nth(a, ST_STEPS, ST_STEPS))
                if negmax_of is not None:
                    pe.wait_ge(sm_read, nth(negmax_of, SM_STEPS, SM_STEPS))
                    for t in range(TT):
                        m = pe.transpose(SX[0:NH, 3, t * 128:(t + 1) * 128], negmax[:, t, :], ident[:, :])
                    m.then_inc(mtr_done, 1)
                if b is not None:
                    down(b)
                if a is not None:
                    pe.wait_ge(o_copied, nth(a, 2, 2))
                    for t in range(TT):
                        for s in range(SET):
                            m = pe.transpose(SX[:, t, s * 128:(s + 1) * 128], o_aug[:, s, t * 128:(t + 1) * 128],
                                             ident[:, :])
                    m.then_inc(otr_done, 1)
                if b is not None:
                    up(b)
                if a is not None:
                    pe.wait_ge(o_ready, nth(a, 1, 1))
                    transpose4(SX[:, 2, :], o_tok).then_inc(ontr_done, 1)
                if b is not None:
                    h1_transpose(b)
                if a is not None:
                    pe.wait_ge(oT_hi, nth(a, 1, 1))
                    pe.wait_ge(oT_lo, nth(a, 1, 1))
                    for t in range(TT):
                        c = slice(t * 128, (t + 1) * 128)
                        m = three(PV[:, 1, t * D:(t + 1) * D],
                                  [(pair(oT, full, k, c), pair(wo, full, k, full)) for k in range(KT)])
                    m.then_inc(wo_done, 1)
                if b is not None:
                    pe.wait_ge(h1T_hi, nth(b, 1, 1))
                    pe.wait_ge(h1T_lo, nth(b, 1, 1))
                    project_qk(b, 0, q_done)
                    project_qk(b, 1, k_done)
                if a is not None:
                    pe.wait_ge(h2_ready, nth(a, 1, 1))
                    transpose4(MM[:, 1, :], h2).then_inc(h2tr_done, 1)
                if b is not None:
                    if negmax_of is not None:
                        pe.wait_ge(negmaxT_ready, nth(negmax_of, 1, 1))
                    project_v(b)
                if a is not None:
                    pe.wait_ge(h2T_hi, nth(a, 1, 1))
                    pe.wait_ge(h2T_lo, nth(a, 1, 1))
                    for m4, bank in enumerate((SX[:, 2], MM[:, 0], MM[:, 1], SX[:, 0])):
                        if m4 == 3 and b is not None:
                            pe.wait_ge(q_hi, nth(b, 1, 1))
                            pe.wait_ge(q_lo, nth(b, 1, 1))
                        for f in range(2):
                            c = slice((2 * m4 + f) * 128, (2 * m4 + f + 1) * 128)
                            m = three(bank[:, f * P:(f + 1) * P],
                                      [(pair(wf1, full, k, c), pair(h2T, full, k, full)) for k in range(KT)])
                        m.then_inc(f1_done, 1)
                    for k in range(FT):
                        if k % 2 == 0:
                            pe.wait_ge(g_lo_done, nth(a, 4, k // 2 + 1))
                        for t in range(TT):
                            c = slice(t * 128, (t + 1) * 128)
                            m = three(PV[:, 0, t * D:(t + 1) * D], [(pair((g_hi, g_lo), full, k, c), pair(wf2, full, k, full))],
                                      first=k == 0 and t == 0, last=k == FT - 1, skip_group_check=True)
                    m.then_inc(f2_done, 1)
                if b is not None:
                    pe.wait_ge(q_lo, nth(b, 1, 1))
                    pe.wait_ge(k_lo, nth(b, 1, 1))
                    pe.wait_ge(v_ready, nth(b, 1, 1))

            def max_step(b, par_, n):
                s, t, j = n // 4, n // 2 % 2, 2 * (n % 2)
                g, half = s // HALF, s % HALF
                if n == 0:
                    pe.wait_ge(q_stacked, nth(b, 96, 96))
                    pe.wait_ge(k_stacked, nth(b, 96, 96))
                if n >= 2:
                    pe.wait_ge(sm_read, nth(b, SM_STEPS, n - 1))
                for p in range(2):
                    m = pe.matmul(MM[:, n % 2, p * P:(p + 1) * P],
                                  q_stack[par_][0:MROW, half, j + p, g, t * 128:(t + 1) * 128],
                                  k_stack[par_][0:MROW, j + p, g, :], start=True, stop=True)
                m.then_inc(sm_done, 1)

            def score_step(b, par_, u):
                s, j = u // 2, 2 * (u % 2)
                g, half = s // HALF, s % HALF
                if u >= 2:
                    pe.wait_ge(exp_done, nth(b, ST_STEPS, u - 1))
                for p in range(2):
                    for t in range(TT):
                        m = pe.matmul(SX[:, j + p, t * P:(t + 1) * P],
                                      k_stack[par_][0:MROW + 1, j + p, g, t * 128:(t + 1) * 128],
                                      q_stack[par_][0:MROW + 1, half, j + p, g, :], start=True, stop=True)
                m.then_inc(st_done, 1)

            def values(b, par_, s):
                pe.wait_ge(exp_done, nth(b, ST_STEPS, 2 * s + 2))
                for t in range(TT):
                    for j in range(PP):
                        m = pe.matmul(PV[32 * j:32 * j + 32, s // 2, s % 2 * P:(s % 2 + 1) * P],
                                      v_aug[par_][:, t, s * PP + j, :], probs[s % 2][:, j, t, :],
                                      start=t == 0, stop=t == TT - 1)
                m.then_inc(pv_done, 1)

            def phase2(i, par_, front=True, tail_of=None):
                if isinstance(i, int) and i == 0:
                    pe.wait_ge(ones_set, 2)
                pe.wait_ge(m_stacked, nth(i, 16, 16))
                for u in range(ST_STEPS):
                    score_step(i, par_, u)
                    if front:
                        max_step(i + 1, 1 - par_, 2 * u)
                        max_step(i + 1, 1 - par_, 2 * u + 1)
                    if u == 0 and tail_of is not None:
                        pe.wait_ge(a2y_ready, nth(tail_of, 1, 1))
                    if u >= 2 and u % 2 == 0:
                        values(i, par_, u // 2 - 1)
                values(i, par_, SET - 1)

            def delta_chunk(n):
                b2, half = n // 2, n % 2
                pe.wait_ge(ld_ring[n % RING], 16 * (n // RING + 1))
                if half == 0 and b2 >= 2:
                    pe.wait_ge(delta_copied, b2 - 1)
                data = ring[:, n % RING, :].rearrange("p (k j n) -> p k j n", k=KH, j=2)
                for k in range(KH):
                    for j in range(2):
                        at = 32 * (2 * half + j)
                        m = pe.matmul(SX[at:at + 32, b2 % 2, :], hbd[:, k, :], data[:, k, j, :],
                                      start=k == 0, stop=k == KH - 1)
                m.then_inc(delta_done, 1)

            def delta_transpose(n):
                pe.wait_ge(delta_copied, n + 1)
                if n >= 2:
                    pe.wait_ge(delta_ready, n - 1)
                for c in range(4):
                    m = pe.transpose(SX[:, 2 + n % 2, c * 128:(c + 1) * 128], dtmp[:, n % 2, c * 128:(c + 1) * 128],
                                     ident[:, :])
                m.then_inc(deltaT_done, 1)

            def columns(bank, tiles, w, x, at=0):
                for c in range(tiles):
                    for k in range(KT):
                        m = pe.matmul(MM[:, bank, c * B:(c + 1) * B], w[:, k, at + c * 128:at + (c + 1) * 128],
                                      x[:, k, :], start=k == 0, stop=k == KT - 1)
                return m

            pe.wait_ge(ld_const, 16 * 4)
            pe.wait_ge(ld_small, 16)
            for f in range(KT):
                m = pe.matmul(MM[:, 0, f * B:(f + 1) * B], wt1[:, f * 128:(f + 1) * 128], cond_t, start=True, stop=True)
            m.then_inc(pe_cond, 1)
            delta_chunk(0)
            pe.wait_ge(act_cond, 1)
            columns(1, KT, wt2, s1).then_inc(pe_cond, 1)
            delta_chunk(1)
            delta_transpose(0)
            delta_chunk(2)
            pe.wait_ge(act_cond, 2)
            pe.wait_ge(ld_wc, 32)
            columns(0, 8, wc, s2).then_inc(pe_cond, 1)
            for k in range(KT):
                m = pe.matmul(MM[0:B, 1, :], s2[:, k, :], wc[:, k, 4 * D:6 * D], start=k == 0, stop=k == KT - 1)
            m.then_inc(pe_cond, 1)
            delta_chunk(3)
            delta_transpose(1)
            delta_chunk(4)
            pe.wait_ge(ld_wqkv, 16)
            pe.wait_ge(dve_cond, 2)
            columns(0, 6, wqkv_f, mod[:, 2:4, :]).then_inc(pe_cond, 1)
            delta_chunk(5)
            delta_transpose(2)
            delta_chunk(6)
            pe.wait_ge(ld_wf1, 16)
            pe.wait_ge(dve_cond, 3)
            columns(1, 8, wf1_f, mod[:, 6:8, :]).then_inc(pe_cond, 1)
            delta_chunk(7)
            for n in range(4, NCHUNK // 2):
                delta_transpose(n - 1)
                delta_chunk(2 * n)
                delta_chunk(2 * n + 1)
            delta_transpose(NCHUNK // 2 - 1)
            pe.wait_ge(dve_cond, 5)
            pe.wait_ge(delta_ready, NCHUNK // 2)
            pe.wait_ge(w_lo, 1)
            phase1(0, 0)
            pe.wait_ge(pool_init, 4)
            for n in range(SM_STEPS):
                max_step(0, 0, n)
            phase1(1, 1, negmax_of=0)
            pe.wait_ge(w_lo, 4)
            phase2(0, 0)
            with pe.Fori(1, B - 2, 2) as i0:
                for u in range(2):
                    i = i0 + u
                    phase1(i + 1, u % 2, negmax_of=i, tail_of=i - 1)
                    phase2(i, (1 + u) % 2, tail_of=i - 1)
            phase1(None, 0, negmax_of=B - 1, tail_of=B - 2)
            phase2(B - 1, 1, front=False, tail_of=B - 2)
            phase1(None, 0, tail_of=B - 1)


def kernel(x, cond_256, fside_BxS_0, L0_cond_Wd, L0_cond_bd, L0_cond_Wu, L0_cond_bu, L0_cond_Wdd, L0_cond_bdd,
           L0_cond_Wdu, L0_cond_bdu, L1_cond_W_t1, L1_cond_b_t1, L1_cond_W_t2, L1_cond_b_t2, L1_cond_W_c,
           L1_cond_b_c, L1_cond_W_qkv, L1_cond_b_qkv, L1_cond_W_o, L1_cond_b_o, L1_cond_W_f1, L1_cond_b_f1,
           L1_cond_W_f2, L1_cond_b_f2):
    import numpy as np
    import concourse.bacc as bacc
    from concourse.bass_utils import run_bass_kernel_spmd as run

    (x, h, c, Wd, bd, Wu, bu, Wdd, bdd, Wdu, bdu, Wt1, bt1, Wt2, bt2, Wc, bc, Wqkv, bqkv, Wo, bo, Wf1, bf1, Wf2,
     bf2) = (np.asarray(a) for a in (
         x, cond_256, fside_BxS_0, L0_cond_Wd, L0_cond_bd, L0_cond_Wu, L0_cond_bu, L0_cond_Wdd, L0_cond_bdd,
         L0_cond_Wdu, L0_cond_bdu, L1_cond_W_t1, L1_cond_b_t1, L1_cond_W_t2, L1_cond_b_t2, L1_cond_W_c,
         L1_cond_b_c, L1_cond_W_qkv, L1_cond_b_qkv, L1_cond_W_o, L1_cond_b_o, L1_cond_W_f1, L1_cond_b_f1,
         L1_cond_W_f2, L1_cond_b_f2))

    def by_tile(w):
        return w.reshape(-1, 128, w.shape[1]).transpose(1, 0, 2)

    def column(v, repeat=1):
        return np.repeat(v.reshape(-1, 128).T, repeat, axis=1)

    cols = np.concatenate([column(bd), column(bt1), column(bt2), by_tile(c.T).reshape(128, -1),
                           column(bc[:4 * D], B), column(bqkv, B), column(bf1, B)], axis=1)
    hbd = np.zeros((4, 32, KH, 4, B), h.dtype)
    for j in range(4):
        hbd[j, :, :, j, :] = h.T.reshape(KH, 32, B).transpose(1, 0, 2)
    small = np.zeros((128, 768 + B), h.dtype)
    small[:HC, 0:256] = Wt1.T
    small[:, 256:768] = by_tile(Wt2.T).reshape(128, -1)
    small[:HC, 768:] = h.T
    def down_columns(w):
        return w.reshape(BN, KT, 128, -1).transpose(2, 1, 0, 3).reshape(128, 2 * 128, -1)

    def up_columns(w):
        return w.reshape(D, BN, -1).transpose(1, 0, 2)
    base = np.concatenate([f(w)[:, :, 0] for w_ in ((Wd, Wu), (bdd, bdu)) for f, w in zip((down_columns, up_columns), w_)],
                          axis=1)
    gen = np.concatenate([down_columns(Wdd), up_columns(Wdu)], axis=1)
    gen = gen.reshape(128, 8, 4, 2, 2, 4, KH, 32).transpose(1, 3, 5, 7, 6, 4, 2, 0).reshape(NCHUNK, 128, CHUNK)

    arrays = {
        "x_tok": x, "x_feat": x.transpose(0, 2, 1), "cols_in": cols, "hbd_in": hbd.reshape(128, KH, 32),
        "ident_in": np.eye(128, dtype=np.float32), "base_in": base, "small_w": small, "wc_in": by_tile(Wc.T),
        "wqkv_in": by_tile(Wqkv.T), "wf1_in": by_tile(Wf1.T), "wdelta_in": gen,
        "wf2_in": by_tile(Wf2.T).reshape(128, -1), "wo_in": by_tile(Wo.T).reshape(128, -1),
        "rows_in": np.broadcast_to(np.stack([bu, bo, bf2]), (128, 3, D)),
        "bcrow_in": np.broadcast_to(bc[4 * D:], (B, 2 * D)),
    }
    arrays = {k: np.ascontiguousarray(v) for k, v in arrays.items()}
    nc = bacc.Bacc("TRN2", target_bir_lowering=False, num_devices=1)
    args = {k: nc.dram_tensor(k, v.shape, mybir.dt.from_np(v.dtype), kind="ExternalInput").ap()
            for k, v in arrays.items()}
    args["out"] = nc.dram_tensor("out", (B, P, D), FP32, kind="ExternalOutput").ap()
    build(nc, **args)
    r = run(nc, [arrays], core_ids=[0])
    return r.results[0]["out"]
```

```python
import concourse.bass as bass
from concourse import mybir
from contextlib import ExitStack

FP32 = mybir.dt.float32
F32R = mybir.dt.float32r
ALU = mybir.AluOpType
ACT = mybir.ActivationFunctionType
AX = mybir.AxisListType

B = 8
P = 256
D = 256
BN = 128
HC = 64
NH, DH = 16, 16
F = 1024
KT = D // 128
TT = P // 128
FT = F // 128
EPS = 1e-5
DELTA_SCALE = 0.1

G, HALF, PP = 2, 2, 4
SET = G * HALF
STK = 3 * DH
MROW = 2 * STK
STACK_DMAS = HALF
STACK_PARTS = ((0, 1, 2), (0, 2, 1))

KH = 2
NCHUNK = 16
CHUNK = 2048
RING = 3

C_BD, C_BT1, C_BT2, C_EMB = 0, 1, 3, 5
C_BC = C_EMB + KT * B
C_BQKV = C_BC + 8 * B
C_BF1 = C_BQKV + 6 * B
C_END = C_BF1 + FT * B

T_G1, T_QB, T_KB, T_VB, T_G2, T_F1 = 0, 2, 4, 6, 8, 10
NPAR = 18
NPAR_A = 6

SM_STEPS = NH // 2 * TT
ST_STEPS = NH
SET_STEPS = ST_STEPS // SET

S_BANKS = 3
B_Q, B_K, B_V = 1, 2, 0
M0, M1 = 3, 4
VAL = 5
X, Y = 6, 7
F1_BANKS = (Y, X, Y, X)


def build(nc, x_tok, x_feat, cols_in, hbd_in, ident_in, base_in, small_w, wc_in, wqkv_in, wf1_in, wdelta_in,
          wf2_in, wo_in, rows_in, bcrow_in, out):
    ctx = ExitStack()
    with ctx:
        def sb(name, shape, dt=FP32):
            return ctx.enter_context(nc.sbuf_tensor(name, shape, dt))

        def sem(name):
            return ctx.enter_context(nc.semaphore(name))

        wqkv = [sb(f"wqkv_{p}", [128, KT, 3 * D], F32R) for p in ("hi", "lo")]
        wo = [sb(f"wo_{p}", [128, KT, D], F32R) for p in ("hi", "lo")]
        wf1 = [sb(f"wf1_{p}", [128, KT, F], F32R) for p in ("hi", "lo")]
        wf2 = [sb(f"wf2_{p}", [128, FT, D], F32R) for p in ("hi", "lo")]
        k_stack = [sb(f"k_stack{i}", [128, PP, G, P], F32R) for i in range(2)]
        q_stack = [sb(f"q_stack{i}", [128, HALF, PP, G, P], F32R) for i in range(2)]
        ring = sb("ring", [128, RING, CHUNK])
        probs = [ring[:, i, :].rearrange("p (j t q) -> p j t q", j=PP, t=TT) for i in range(2)]
        gelu_f = ring[:, 0, :].rearrange("p (f n) -> p f n", f=FT)
        a2y, h2T_f = [ring[:, 2, i * 512:(i + 1) * 512].rearrange("p (k n) -> p k n", k=KT) for i in (2, 3)]
        x2 = [ring[:, 2, i * 512:(i + 1) * 512].rearrange("p (t n) -> p t n", t=TT) for i in range(2)]
        g_hi = sb("g_hi", [128, FT, P], F32R)
        g_lo = sb("g_lo", [128, FT, P], F32R)
        qk_parts = g_hi[:, :, :].rearrange("p (w h g) n -> p w h g n", w=2, h=2)
        arena = sb("arena", [128, 6656])
        wc = arena[:, 0:3072].rearrange("p (k n) -> p k n", k=KT)
        wqkv_f = arena[:, 3072:4608].rearrange("p (k n) -> p k n", k=KT)
        wt1 = arena[0:HC, 4608:4864]
        wt2 = arena[:, 4864:5376].rearrange("p (k n) -> p k n", k=KT)
        cond_t = arena[0:HC, 5376:5376 + B]
        wf1_f = ring[:, NCHUNK % RING, :].rearrange("p (k n) -> p k n", k=KT)

        def tile(at):
            return arena[:, at:at + 512].rearrange("p (t n) -> p t n", t=2)
        x_in = [tile(0), tile(512)]
        h1T_f = tile(1024)
        xT = tile(1536)
        h1 = tile(2048)
        h2 = tile(2560)
        o_tok = tile(3072)
        a12 = [tile(3584), tile(4096)]
        v_aug = [arena[:, 4608 + i * 1024:5632 + i * 1024].rearrange("p (t h n) -> p t h n", t=TT, h=NH)
                 for i in range(2)]
        o_aug = sb("o_aug", [128, SET, P])
        dtmp = o_aug[:, :, :].rearrange("p (i s) n -> p i (s n)", i=2)
        w_ad = sb("w_ad", [128, B, 2 * D])
        base = sb("base", [128, 1024])
        downT = base[:, 512:768]
        wd_cur = base[:, 768:1024].rearrange("p (k n) -> p k n", k=KT)
        a1bo = base[:, 0:256]
        a2bf2 = base[:, 256:512]
        h1T = [sb(f"h1T_{p}", [128, KT, P], F32R) for p in ("hi", "lo")]
        h2T = [sb(f"h2T_{p}", [128, KT, P], F32R) for p in ("hi", "lo")]
        oT = [sb(f"oT_{p}", [128, KT, P], F32R) for p in ("hi", "lo")]
        ident = sb("ident", [128, 128])
        hbd = sb("hbd", [128, KH, 32])
        cols = sb("cols", [128, C_END])
        rows = sb("rows", [128, 3, D])
        par = sb("par", [128, B, NPAR])
        par_a = sb("par_a", [128, NPAR_A])
        par_t = [sb(f"par_t{i}", [128, NPAR - NPAR_A]) for i in range(2)]
        s1 = sb("s1", [128, KT, B])
        z2 = sb("z2", [128, KT, B])
        s2 = sb("s2", [128, KT, B])
        mod = sb("mod", [128, 8, B])
        negmax = sb("negmax", [128, TT, NH])
        negmaxT = sb("negmaxT", [NH, P], F32R)
        rden = sb("rden", [128, TT, NH])
        neghalf = sb("neghalf", [128, TT])
        eps = sb("eps", [128, TT])
        bn1 = sb("bn1", [128, TT, 6])
        bn2 = sb("bn2", [128, TT, 6])
        mv1 = sb("mv1", [128, TT, 2])
        mv2 = sb("mv2", [128, TT, 2])
        ve1 = sb("ve1", [128, TT])
        ve2 = sb("ve2", [128, TT])
        rs1 = sb("rs1", [128, TT])
        rs2 = sb("rs2", [128, TT])
        a_sb = sb("a_sb", [B, 2 * D])
        scrap = sb("scrap", [128, 2])

        PS = ctx.enter_context(nc.psum_tensor("PS", [128, 8, 512], FP32))

        def bank(n):
            return PS[:, n, :]

        qk_scr = nc.dram_tensor("qk_scr", (2, HALF * PP, 3, DH, G * P), FP32).ap()
        a_scr = nc.dram_tensor("a_scr", (B, 2 * D), FP32).ap()
        x1_scr = nc.dram_tensor("x1_scr", (B, P, D), FP32).ap()

        (ld_const, ld_small, ld_wc, ld_wqkv, ld_wf1, ld_x, ld_xT, ld_a12, stored, a_saved) = map(sem, (
            "ld_const", "ld_small", "ld_wc", "ld_wqkv", "ld_wf1", "ld_x", "ld_xT", "ld_a12", "stored", "a_saved"))
        (ld_rows, ld_x2, x1_saved, h1T_f_ready, h2T_f_ready) = map(sem, (
            "ld_rows", "ld_x2", "x1_saved", "h1T_f_ready", "h2T_f_ready"))
        ld_ring = [sem(f"ld_ring{i}") for i in range(RING)]
        (delta_done, delta_copied, deltaT_done, delta_ready) = map(sem, (
            "delta_done", "delta_copied", "deltaT_done", "delta_ready"))
        (pe_cond, act_cond, dve_cond, w_hi, w_lo, init_done, pool_init, ones_set) = map(sem, (
            "pe_cond", "act_cond", "dve_cond", "w_hi", "w_lo", "init_done", "pool_init",
            "ones_set"))
        (xb_ready, wd_ready, pa_ready, pt_ready, down_done, relu_ready, up_done, x1_ready, st1_ready, rs1_ready,
         h1_ready, h1tr_done, h1T_hi, h1T_lo, q_done, q_hi, q_lo, k_done, k_hi, k_lo, v_done, v_ready) = map(sem, (
            "xb_ready", "wd_ready", "pa_ready", "pt_ready", "down_done", "relu_ready", "up_done", "x1_ready",
            "st1_ready", "rs1_ready", "h1_ready", "h1tr_done", "h1T_hi", "h1T_lo", "q_done", "q_hi", "q_lo",
            "k_done", "k_hi", "k_lo", "v_done", "v_ready"))
        (q_saved, k_saved, q_stacked, k_stacked, sm_done, sm_read, mtr_done, negmaxT_ready, m_stacked, st_done,
         exp_done, pv_done, o_copied, otr_done, rden_ready, o_ready, ontr_done, oT_hi, oT_lo, wo_done) = map(sem, (
            "q_saved", "k_saved", "q_stacked", "k_stacked", "sm_done", "sm_read", "mtr_done", "negmaxT_ready",
            "m_stacked", "st_done", "exp_done", "pv_done", "o_copied", "otr_done", "rden_ready", "o_ready",
            "ontr_done", "oT_hi", "oT_lo", "wo_done"))
        (abias_ready, x2base_ready, a1o_ready, x2_ready, st2_ready, rs2_ready, h2_ready, x2b_ready, h2tr_done, h2T_hi,
         h2T_lo, f1_done, gelu_done, g_hi_done, g_lo_done, f2_done, a2y_ready, x3_ready, ve1_ready, ve2_ready,
         bns1_ready, bns2_ready) = map(sem, (
            "abias_ready", "x2base_ready", "a1o_ready", "x2_ready", "st2_ready", "rs2_ready", "h2_ready", "x2b_ready",
            "h2tr_done", "h2T_hi", "h2T_lo", "f1_done", "gelu_done", "g_hi_done", "g_lo_done", "f2_done",
            "a2y_ready", "x3_ready", "ve1_ready", "ve2_ready",
            "bns1_ready", "bns2_ready"))

        def nth(b, n, k):
            return b * n + k

        def real(b):
            return not isinstance(b, int) or 0 <= b < B

        def later(b, n=1):
            return not isinstance(b, int) or b >= n

        def one(b):
            return b.unsqueeze(1).to_broadcast([128, TT, D])

        block = ctx.enter_context(nc.Block())

        @block.sync
        def _(sp):
            def load_chunk(n):
                if n >= RING:
                    if n - RING < NCHUNK:
                        sp.wait_ge(delta_done, n - RING + 1)
                src = wdelta_in[n] if n < NCHUNK else (wf1_in, wf2_in, wo_in)[n - NCHUNK]
                sp.dma_start(ring[:, n % RING, 0:src.shape[1]], src).then_inc(ld_ring[n % RING], 16)

            def load_front(b, par_):
                if later(b):
                    sp.wait_ge(down_done, nth(b, 1, 0))
                sp.dma_start(xT, x_feat[bass.ds(b, 1)].rearrange("o (k p) n -> p (o k) n", p=128)).then_inc(ld_xT, 16)
                if later(b, 2):
                    sp.wait_ge(x1_saved, nth(b - 1, 16, 0))
                    sp.wait_ge(h1_ready, nth(b - 1, 1, 0))
                sp.dma_start(x_in[par_], x_tok[bass.ds(b, 1)].rearrange("o (t p) n -> p (o t) n", p=128))\
                  .then_inc(ld_x, 16)

            def save_x1(b, par_):
                sp.wait_ge(x1_ready, nth(b, 1, 1))
                sp.dma_start(x1_scr[bass.ds(b, 1)].rearrange("o (t p) n -> p (o t) n", p=128), x_in[par_])\
                  .then_inc(x1_saved, 16)

            def store(b, par_):
                sp.wait_ge(x3_ready, nth(b, 1, 1))
                sp.dma_start(out[bass.ds(b, 1)].rearrange("o (t p) n -> p (o t) n", p=128), x2[par_])\
                  .then_inc(stored, 16)

            def load_residual(b, par_):
                if later(b, 2):
                    sp.wait_ge(stored, nth(b - 1, 16, 0))
                if later(b):
                    sp.wait_ge(x2base_ready, nth(b, 1, 0))
                if not real(b + 2):
                    sp.wait_ge(x1_saved, nth(b, 16, 16))
                sp.dma_start(x2[par_], x1_scr[bass.ds(b, 1)].rearrange("o (t p) n -> p (o t) n", p=128))\
                  .then_inc(ld_x2, 16)
                sp.dma_start(a12[par_].rearrange("p t n -> p (t n)"),
                             a_scr[bass.ds(b, 1), :].to_broadcast([128, 2 * D])).then_inc(ld_a12, 16)

            def save_qk(b, w, hi, lo, saved, stacked):
                if later(b):
                    sp.wait_ge(stacked, nth(b, STACK_DMAS * 16, 0))
                first, second, last = STACK_PARTS[w]
                sp.wait_ge(hi, nth(b, 1, 1))
                for part in (first, second):
                    sp.dma_start(qk_scr[w, :, part], qk_parts[:, w, 0].rearrange("p g n -> p (g n)").bitcast(FP32))\
                      .then_inc(saved, 16)
                sp.wait_ge(lo, nth(b, 1, 1))
                sp.dma_start(qk_scr[w, :, last], qk_parts[:, w, 1].rearrange("p g n -> p (g n)").bitcast(FP32))\
                  .then_inc(saved, 16)

            def stack(b, w, dst, saved, done):
                sp.wait_ge(saved, nth(b, 48, 48))
                for half in range(HALF):
                    at = half * STK
                    to = dst[at:at + STK, half] if w == 0 else dst[at:at + STK]
                    sp.dma_start(to.rearrange("r j g n -> r j (g n)").bitcast(FP32),
                                 qk_scr[w, half * PP:(half + 1) * PP].rearrange("j part d n -> (part d) j n"))\
                      .then_inc(done, 16)

            def phase1(i, par_):
                if real(i + 2):
                    load_front(i + 2, par_)
                if real(i + 1):
                    save_qk(i + 1, 0, q_hi, q_lo, q_saved, q_stacked)
                if real(i):
                    sp.wait_ge(negmaxT_ready, nth(i, 1, 1))
                    sp.dma_start(q_stack[par_][MROW:MROW + 1].rearrange("o a j g n -> o (a j g) n").bitcast(FP32),
                                 negmaxT[:, :].bitcast(FP32)).then_inc(m_stacked, 16)
                if real(i + 1):
                    save_qk(i + 1, 1, k_hi, k_lo, k_saved, k_stacked)
                    stack(i + 1, 0, q_stack[1 - par_], q_saved, q_stacked)
                    stack(i + 1, 1, k_stack[1 - par_], k_saved, k_stacked)

            def phase2(i, par_):
                if real(i - 2):
                    store(i - 2, par_)
                if real(i):
                    load_residual(i, par_)
                if real(i + 2):
                    save_x1(i + 2, par_)

            sp.dma_start(cols[:, :], cols_in).then_inc(ld_const, 16)
            sp.dma_start(hbd[:, :, :], hbd_in).then_inc(ld_const, 16)
            sp.dma_start(arena[:, 4608:5376 + B], small_w).then_inc(ld_small, 16)
            load_chunk(0)
            sp.dma_start(base[:, :], base_in).then_inc(ld_const, 16)
            sp.dma_start(ident[:, :], ident_in).then_inc(ld_const, 16)
            load_chunk(1)
            sp.dma_start(wc, wc_in).then_inc(ld_wc, 16)
            sp.dma_start(a_sb[:, :], bcrow_in).then_inc(ld_wc, 16)
            load_chunk(2)
            sp.dma_start(wqkv_f, wqkv_in).then_inc(ld_wqkv, 16)
            for n in range(3, 8):
                load_chunk(n)
            sp.dma_start(rows[:, :, :], rows_in).then_inc(ld_rows, 16)
            for n in range(8, NCHUNK):
                load_chunk(n)
                if n == 9:
                    sp.wait_ge(pe_cond, 4)
                    load_front(0, 0)
                if n == 13:
                    load_front(1, 1)
            for n in range(NCHUNK, NCHUNK + 3):
                load_chunk(n)
            sp.wait_ge(dve_cond, 3)
            sp.dma_start(a_scr, a_sb[:, :]).then_inc(a_saved, 16)
            save_x1(0, 0)
            save_qk(0, 0, q_hi, q_lo, q_saved, q_stacked)
            save_qk(0, 1, k_hi, k_lo, k_saved, k_stacked)
            sp.wait_ge(pool_init, 5)
            stack(0, 0, q_stack[0], q_saved, q_stacked)
            stack(0, 1, k_stack[0], k_saved, k_stacked)
            load_front(2, 0)
            save_x1(1, 1)
            save_qk(1, 0, q_hi, q_lo, q_saved, q_stacked)
            save_qk(1, 1, k_hi, k_lo, k_saved, k_stacked)
            stack(1, 0, q_stack[1], q_saved, q_stacked)
            stack(1, 1, k_stack[1], k_saved, k_stacked)
            sp.wait_ge(negmaxT_ready, 1)
            sp.dma_start(q_stack[0][MROW:MROW + 1].rearrange("o a j g n -> o (a j g) n").bitcast(FP32),
                         negmaxT[:, :].bitcast(FP32)).then_inc(m_stacked, 16)
            sp.wait_ge(a_saved, 16)
            sp.wait_ge(w_lo, 4)
            phase2(0, 0)
            phase1(1, 1)
            phase2(1, 1)
            with sp.Fori(2, B - 3, 2) as j:
                for u in range(2):
                    phase1(j + u, u)
                    phase2(j + u, u)
            for i in range(B - 2, B + 2):
                phase1(i, i % 2)
                phase2(i, i % 2)
            sp.wait_ge(stored, 16 * B)

        @block.gpsimd
        def _(pool):
            def rstd(b, st_ready, mv, ve, ve_ready, rs, rs_ready):
                pool.wait_ge(st_ready, nth(b, 1, 1))
                pool.tensor_tensor(ve[:, :], mv[:, :, 1], eps[:, :], ALU.add).then_inc(ve_ready, 1)
                pool.wait_ge(ve_ready, nth(b, 1, 1))
                pool.tensor_tensor(rs[:, :], ve[:, :], neghalf[:, :], ALU.pow).then_inc(rs_ready, 1)

            def biased(b, par_):
                pool.wait_ge(ld_x, nth(b, 16, 16))
                pool.tensor_tensor(x_in[par_], x_in[par_], one(rows[:, 0, :]), ALU.add).then_inc(xb_ready, 1)

            def rstd_front(b):
                rstd(b, st1_ready, mv1, ve1, ve1_ready, rs1, rs1_ready)

            def residual(b, par_):
                if later(b):
                    pool.wait_ge(x2b_ready, nth(b, 1, 0))
                pool.wait_ge(ld_a12, nth(b, 16, 16))
                pool.tensor_tensor(a1bo, a12[par_][:, 0, :], rows[:, 1, :], ALU.mult).then_inc(abias_ready, 1)
                pool.tensor_tensor(a2bf2, a12[par_][:, 1, :], rows[:, 2, :], ALU.mult).then_inc(abias_ready, 1)
                pool.wait_ge(ld_x2, nth(b, 16, 16))
                pool.wait_ge(abias_ready, nth(b, 2, 1))
                pool.tensor_tensor(x2[par_], x2[par_], one(a1bo), ALU.add).then_inc(x2base_ready, 1)

            def residual_end(b, par_):
                rstd(b, st2_ready, mv2, ve2, ve2_ready, rs2, rs2_ready)
                pool.wait_ge(h2_ready, nth(b, 1, 1))
                pool.wait_ge(abias_ready, nth(b, 2, 2))
                pool.tensor_tensor(x2[par_], x2[par_], one(a2bf2), ALU.add).then_inc(x2b_ready, 1)

            def mlp_end(c, par_):
                pool.wait_ge(a2y_ready, nth(c, 1, 1))
                pool.wait_ge(x2b_ready, nth(c, 1, 1))
                pool.tensor_tensor(x2[par_], x2[par_], a2y, ALU.add).then_inc(x3_ready, 1)

            def low(b, lo, whole, hi, ready, lo_ready):
                pool.wait_ge(ready, nth(b, 1, 1))
                pool.tensor_tensor(lo[:, :, :], whole, hi[:, :, :].bitcast(FP32), ALU.subtract).then_inc(lo_ready, 1)

            def phase1(i, par_):
                if real(i - 1):
                    residual(i - 1, 1 - par_)
                if real(i + 2):
                    biased(i + 2, par_)
                if real(i - 1):
                    residual_end(i - 1, 1 - par_)

            def phase2(i, par_):
                if real(i - 2):
                    mlp_end(i - 2, par_)
                if real(i - 1):
                    low(i - 1, h2T[1], h2T_f, h2T[0], h2T_f_ready, h2T_lo)
                if real(i + 2):
                    rstd_front(i + 2)
                    low(i + 2, h1T[1], h1T_f, h1T[0], h1T_f_ready, h1T_lo)

            pool.memset(neghalf[:, :], -0.5).then_inc(pool_init, 1)
            pool.memset(scrap[:, :], 0.0).then_inc(pool_init, 1)
            pool.memset(eps[:, :], EPS).then_inc(pool_init, 1)
            for i in range(2):
                pool.memset(q_stack[i][:, :, :, :, :].bitcast(FP32), 0.0).then_inc(pool_init, 1)
            pool.wait_ge(ld_rows, 16)
            pool.wait_ge(pool_init, 5)
            biased(0, 0)
            biased(1, 1)
            rstd_front(0)
            rstd_front(1)
            low(0, h1T[1], h1T_f, h1T[0], h1T_f_ready, h1T_lo)
            low(1, h1T[1], h1T_f, h1T[0], h1T_f_ready, h1T_lo)
            biased(2, 0)
            phase2(0, 0)
            phase1(1, 1)
            phase2(1, 1)
            with pool.Fori(2, B - 3, 2) as j:
                for u in range(2):
                    phase1(j + u, u)
                    phase2(j + u, u)
            for i in range(B - 2, B + 2):
                phase1(i, i % 2)
                phase2(i, i % 2)

        @block.scalar
        def _(act):
            def relu(b, at):
                act.wait_ge(down_done, nth(b, 1, 1))
                if isinstance(b, int) and b == 1:
                    act.wait_ge(up_done, 1)
                act.activation(downT, PS[:, at, 0:P], ACT.Relu, bias=cols[:, C_BD:C_BD + 1]).then_inc(relu_ready, 1)

            def tiles(out, at, func, column=None, scale=False):
                for f in range(KT):
                    kw = {} if column is None else {"scale" if scale else "bias": column(f)}
                    last = act.activation(out[:, f, :], PS[:, at, f * P:(f + 1) * P], func, **kw)
                return last

            def h1T_high(b, at):
                act.wait_ge(h1tr_done, nth(b, 1, 1))
                act.wait_ge(pa_ready, nth(b, 1, 1))
                for out_, done in ((h1T[0], h1T_hi), (h1T_f, h1T_f_ready)):
                    tiles(out_, at, ACT.Copy, lambda f: par_a[:, T_G1 + f:T_G1 + f + 1], scale=True).then_inc(done, 1)

            def h2T_high(b, par_):
                act.wait_ge(h2tr_done, nth(b, 1, 1))
                for out_, done in ((h2T[0], h2T_hi), (h2T_f, h2T_f_ready)):
                    tiles(out_, Y, ACT.Copy, lambda f: par_t[par_][:, T_G2 - NPAR_A + f:T_G2 - NPAR_A + f + 1],
                          scale=True).then_inc(done, 1)

            def q_high(b):
                act.wait_ge(q_done, nth(b, 1, 1))
                if later(b):
                    act.wait_ge(q_saved, nth(b, 48, 0))
                tiles(qk_parts[:, 0, 0], B_Q, ACT.Identity, lambda f: par_a[:, T_QB + f:T_QB + f + 1]).then_inc(q_hi, 1)

            def k_high(b):
                act.wait_ge(k_done, nth(b, 1, 1))
                if later(b):
                    act.wait_ge(k_saved, nth(b, 48, 0))
                tiles(qk_parts[:, 1, 0], B_K, ACT.Identity, lambda f: par_a[:, T_KB + f:T_KB + f + 1]).then_inc(k_hi, 1)

            def copy_v(b, par_):
                act.wait_ge(v_done, nth(b, 1, 1))
                for t in range(TT):
                    last = act.activation(v_aug[par_][:, t, :, 0:DH],
                                          PS[:, B_V, t * D:(t + 1) * D].rearrange("p (h n) -> p h n", n=DH), ACT.Copy)
                last.then_inc(v_ready, 1)

            def copy_negmax(i):
                act.wait_ge(mtr_done, nth(i, 1, 1))
                if later(i):
                    act.wait_ge(m_stacked, nth(i, 16, 0))
                act.activation(negmaxT[:, :], PS[0:NH, X, 0:P], ACT.Copy).then_inc(negmaxT_ready, 1)

            def copy_o(i, pair_):
                act.wait_ge(pv_done, nth(i, SET, 2 * pair_ + 2))
                act.activation(o_aug[:, 2 * pair_:2 * pair_ + 2, :].rearrange("p s n -> p (s n)"), bank(VAL), ACT.Copy)\
                   .then_inc(o_copied, 1)

            def table(func):
                act.activation(scrap[:, 1:2], scrap[:, 0:1], func)

            def phase1(i, par_):
                b, a, c = i + 1, i - 1, i - 2
                if real(b):
                    q_high(b)
                if real(a):
                    copy_o(a, 1)
                if real(i):
                    copy_negmax(i)
                if real(c):
                    table(ACT.Gelu_apprx_tanh)
                if real(b):
                    k_high(b)
                    copy_v(b, 1 - par_)
                if real(a):
                    act.wait_ge(ontr_done, nth(a, 1, 1))
                    act.wait_ge(pt_ready, nth(a, 1, 1))
                    tiles(oT[0], M0, ACT.Identity, lambda f: par_t[1 - par_][:, f:f + 1]).then_inc(oT_hi, 1)
                if real(c):
                    for m in range(4):
                        act.wait_ge(f1_done, nth(c, 4, m + 1))
                        for f in range(2):
                            col = T_F1 - NPAR_A + 2 * m + f
                            last = act.activation(gelu_f[:, 2 * m + f, :], PS[:, F1_BANKS[m], f * P:(f + 1) * P],
                                                  ACT.Gelu_apprx_tanh, bias=par_t[par_][:, col:col + 1])
                        last.then_inc(gelu_done, 1)
                    if real(i):
                        table(ACT.Exp)

            def phase2(i, par_):
                a, c = i - 1, i - 2
                if not real(i):
                    if real(a):
                        h2T_high(a, 1 - par_)
                    return
                if real(c):
                    act.wait_ge(g_lo_done, nth(c, 4, 4))
                for n in range(ST_STEPS):
                    s, j = n // SET_STEPS, n % SET_STEPS
                    act.wait_ge(st_done, nth(i, ST_STEPS, n + 1))
                    if s >= 2 and j == 0:
                        act.wait_ge(pv_done, nth(i, SET, s - 1))
                    act.activation(probs[s % 2][:, j].rearrange("p t q -> p (t q)"), bank(n % S_BANKS), ACT.Exp,
                                   scale=DH ** -0.5).then_inc(exp_done, 1)
                    if n == 0 and real(i + 2):
                        relu(i + 2, X)
                    if n == 3 and real(a):
                        h2T_high(a, 1 - par_)
                    if n == 11:
                        copy_o(i, 0)
                    if n == 10 and real(i + 2):
                        h1T_high(i + 2, X)

            def copy_delta(n):
                act.wait_ge(delta_done, 2 * n + 2)
                if n >= 2:
                    act.wait_ge(deltaT_done, n - 1)
                act.activation(dtmp[:, n % 2, :], bank(n % 2), ACT.Copy).then_inc(delta_copied, 1)

            def weights_high(n, w):
                act.wait_ge(ld_ring[n % RING], 16 * (n // RING + 1))
                size = w[0].shape[1] * w[0].shape[2]
                act.activation(w[0][:, :, :].rearrange("p k n -> p (k n)"), ring[:, n % RING, 0:size], ACT.Copy)\
                   .then_inc(w_hi, 1)

            act.wait_ge(ld_const, 16 * 4)
            act.wait_ge(pe_cond, 1)
            for f in range(KT):
                last = act.activation(s1[:, f, :], PS[:, M1, f * B:(f + 1) * B], ACT.Silu,
                                      bias=cols[:, C_BT1 + f:C_BT1 + f + 1])
            last.then_inc(act_cond, 1)
            act.wait_ge(dve_cond, 1)
            act.activation(s2[:, :, :], z2[:, :, :], ACT.Silu).then_inc(act_cond, 1)
            copy_delta(0)
            copy_delta(1)
            act.wait_ge(ld_wqkv, 16)
            act.activation(wqkv[0][:, :, :], wqkv_f, ACT.Copy).then_inc(w_hi, 1)
            for n in range(2, NCHUNK // 2):
                copy_delta(n)
                if n == 5:
                    relu(0, X)
            relu(1, Y)
            h1T_high(0, X)
            q_high(0)
            k_high(0)
            copy_v(0, 0)
            h1T_high(1, Y)
            weights_high(NCHUNK, wf1)
            q_high(1)
            k_high(1)
            copy_v(1, 1)
            weights_high(NCHUNK + 1, wf2)
            weights_high(NCHUNK + 2, wo)
            copy_negmax(0)
            act.wait_ge(pool_init, 5)
            act.wait_ge(w_lo, 4)
            phase2(0, 0)
            phase1(1, 1)
            phase2(1, 1)
            with act.Fori(2, B - 3, 2) as j:
                for u in range(2):
                    phase1(j + u, u)
                    phase2(j + u, u)
            for i in range(B - 2, B + 2):
                phase1(i, i % 2)
                phase2(i, i % 2)

        @block.vector
        def _(dve):
            def cut(lo, x, hi):
                return dve.tensor_tensor(lo, x, hi.bitcast(FP32), ALU.subtract)

            def stats(b, x, ready, bn, bn_ready, mv, st_ready):
                dve.wait_ge(ready, nth(b, 1, 1))
                for t in range(TT):
                    last = dve.bn_stats(bn[:, t, :], x[:, t, :])
                last.then_inc(bn_ready, 1)
                dve.wait_ge(init_done, 1)
                dve.wait_ge(bn_ready, nth(b, 1, 1))
                for t in range(TT):
                    last = dve.bn_aggr(mv[:, t, :], bn[:, t, :])
                last.then_inc(st_ready, 1)

            def normalise(b, h, x, mv, rs, rs_ready, h_ready):
                dve.wait_ge(rs_ready, nth(b, 1, 1))
                for t in range(TT):
                    last = dve.tensor_scalar(h[:, t, :], x[:, t, :], mv[:, t, 0:1], rs[:, t:t + 1],
                                             ALU.subtract, ALU.mult)
                last.then_inc(h_ready, 1)

            def low_part(b, hi_ready, lo_ready, lo, hi, at, column, op):
                dve.wait_ge(hi_ready, nth(b, 1, 1))
                for f in range(KT):
                    last = dve.scalar_tensor_tensor(lo[:, f, :], PS[:, at, f * P:(f + 1) * P], column(f),
                                                    hi[:, f, :].bitcast(FP32), op, ALU.subtract)
                last.then_inc(lo_ready, 1)

            def adapter_down(b):
                if later(b):
                    dve.wait_ge(down_done, nth(b, 1, 0))
                dve.tensor_copy(wd_cur, w_ad[:, bass.ds(b, 1), 0:D].rearrange("p o (k n) -> p (o k) n", k=KT))\
                   .then_inc(wd_ready, 1)

            def parameters_a(b):
                if later(b):
                    dve.wait_ge(k_hi, nth(b, 1, 0))
                    dve.wait_ge(k_lo, nth(b, 1, 0))
                dve.tensor_copy(par_a[:, :], par[:, bass.ds(b, 1), 0:NPAR_A].rearrange("p o n -> p (o n)"))\
                   .then_inc(pa_ready, 1)

            def x1_sum(b, par_, at):
                dve.wait_ge(up_done, nth(b, 1, 1))
                dve.wait_ge(xb_ready, nth(b, 1, 1))
                dve.tensor_tensor(x_in[par_], bank(at).rearrange("p (t n) -> p t n", t=TT), x_in[par_], ALU.add)\
                   .then_inc(x1_ready, 1)

            def stats1(b, par_):
                stats(b, x_in[par_], x1_ready, bn1, bns1_ready, mv1, st1_ready)

            def norm1(b, par_):
                if later(b):
                    dve.wait_ge(h1tr_done, nth(b, 1, 0))
                normalise(b, h1, x_in[par_], mv1, rs1, rs1_ready, h1_ready)

            def q_low(b):
                low_part(b, q_hi, q_lo, qk_parts[:, 0, 1], qk_parts[:, 0, 0], B_Q,
                         lambda f: par_a[:, T_QB + f:T_QB + f + 1], ALU.add)

            def k_low(b):
                low_part(b, k_hi, k_lo, qk_parts[:, 1, 1], qk_parts[:, 1, 0], B_K,
                         lambda f: par_a[:, T_KB + f:T_KB + f + 1], ALU.add)

            def o_divided(a, par_):
                dve.wait_ge(otr_done, nth(a, 1, 1))
                o4 = PS[:, M0:M0 + 2, :].rearrange("p t (h n) -> p t h n", n=32)
                dve.reciprocal(rden[:, :, :], o4[:, :, :, DH]).then_inc(rden_ready, 1)
                dve.wait_ge(rden_ready, nth(a, 1, 1))
                for t in range(TT):
                    last = dve.tensor_tensor(o_tok[:, t, :].rearrange("p (h n) -> p h n", n=DH), o4[:, t, :, 0:DH],
                                             rden[:, t, :].unsqueeze(2).to_broadcast([128, NH, DH]), ALU.mult)
                last.then_inc(o_ready, 1)

            def residual(a, par_):
                dve.wait_ge(wo_done, nth(a, 1, 1))
                dve.wait_ge(x2base_ready, nth(a, 1, 1))
                dve.tensor_tensor(h2, bank(M1).rearrange("p (t n) -> p t n", t=TT), one(a12[par_][:, 0, :]), ALU.mult)\
                   .then_inc(a1o_ready, 1)
                dve.wait_ge(a1o_ready, nth(a, 1, 1))
                dve.tensor_tensor(x2[par_], x2[par_], h2, ALU.add).then_inc(x2_ready, 1)

            def gelu_cut(c, m):
                dve.wait_ge(gelu_done, nth(c, 4, m + 1))
                two = slice(2 * m, 2 * m + 2)
                dve.tensor_copy(g_hi[:, two, :], gelu_f[:, two, :]).then_inc(g_hi_done, 1)
                dve.wait_ge(g_hi_done, nth(c, 4, m + 1))
                cut(g_lo[:, two, :], gelu_f[:, two, :], g_hi[:, two, :]).then_inc(g_lo_done, 1)

            def mlp_end(c, par_):
                dve.wait_ge(f2_done, nth(c, 1, 1))
                if later(c):
                    dve.wait_ge(x3_ready, nth(c, 1, 0))
                dve.tensor_tensor(a2y, bank(VAL).rearrange("p (t n) -> p t n", t=TT), one(a12[par_][:, 1, :]), ALU.mult)\
                   .then_inc(a2y_ready, 1)

            def phase1(i, par_):
                b, a, c = i + 1, i - 1, i - 2
                if real(b):
                    q_low(b)
                if real(a):
                    if later(a, 2):
                        dve.wait_ge(gelu_done, nth(a - 1, 4, 0))
                    dve.tensor_copy(par_t[1 - par_][:, :], par[:, bass.ds(a, 1), NPAR_A:NPAR].rearrange("p o n -> p (o n)"))\
                       .then_inc(pt_ready, 1)
                if real(a):
                    o_divided(a, 1 - par_)
                if real(b):
                    k_low(b)
                if real(a):
                    low_part(a, oT_hi, oT_lo, oT[1], oT[0], M0, lambda f: par_t[1 - par_][:, f:f + 1], ALU.add)
                if real(c):
                    if real(b):
                        dve.wait_ge(q_saved, nth(b, 48, 48))
                    gelu_cut(c, 0)
                if real(a):
                    residual(a, 1 - par_)
                if real(c):
                    gelu_cut(c, 1)
                if real(a):
                    stats(a, x2[1 - par_], x2_ready, bn2, bns2_ready, mv2, st2_ready)
                if real(c):
                    if real(b):
                        dve.wait_ge(k_saved, nth(b, 48, 48))
                    gelu_cut(c, 2)
                if real(a):
                    normalise(a, h2, x2[1 - par_], mv2, rs2, rs2_ready, h2_ready)
                if real(c):
                    gelu_cut(c, 3)
                if real(i + 2):
                    adapter_down(i + 2)
                    parameters_a(i + 2)

            def row_max(b, n):
                s, t, j = n // 4, n // 2 % 2, 2 * (n % 2)
                g, half = s // HALF, s % HALF
                at = half * PP * G + j * G + g
                dve.wait_ge(sm_done, nth(b, SM_STEPS, n + 1))
                dve.tensor_reduce(negmax[:, t, at:at + G + 1:G], bank(M0 + n % 2).rearrange("p (j n) -> p j n", j=2),
                                  AX.X, ALU.max, negate=True).then_inc(sm_read, 1)

            def phase2(i, par_):
                a, c = i - 1, i - 2
                if real(c):
                    mlp_end(c, par_)
                for n in range(SM_STEPS):
                    if real(i + 1):
                        row_max(i + 1, n)
                    if real(i + 2):
                        if n == 4:
                            x1_sum(i + 2, par_, X)
                        if n == 5:
                            stats1(i + 2, par_)
                        if n == 7:
                            norm1(i + 2, par_)

            for i in range(2):
                dve.memset(k_stack[i][MROW:MROW + 1].bitcast(FP32), 1.0).then_inc(ones_set, 1)
            dve.wait_ge(ld_const, 16 * 4)
            dve.wait_ge(pe_cond, 2)
            for f in range(KT):
                last = dve.scalar_tensor_tensor(z2[:, f, :], PS[:, VAL, f * B:(f + 1) * B], cols[:, C_BT2 + f:C_BT2 + f + 1],
                                                cols[:, C_EMB + f * B:C_EMB + (f + 1) * B], ALU.add, ALU.add)
            last.then_inc(dve_cond, 1)

            def add_delta(n):
                w = n // 4
                if n == 0:
                    dve.scalar_tensor_tensor(base[:, 0:512], base[:, 512:1024], DELTA_SCALE, base[:, 0:512],
                                             ALU.mult, ALU.add).then_inc(init_done, 1)
                    dve.wait_ge(init_done, 1)
                dve.wait_ge(deltaT_done, n + 1)
                c0 = n * 64
                dve.scalar_tensor_tensor(w_ad[:, :, c0:c0 + 64].rearrange("p b c -> p c b"),
                                         bank(2 + n % 2).rearrange("p (c b) -> p c b", b=B), DELTA_SCALE,
                                         base[:, c0:c0 + 64].unsqueeze(2).to_broadcast([128, 64, B]),
                                         ALU.mult, ALU.add).then_inc(delta_ready, 1)

            def weights_low(n, w):
                size = w[0].shape[1] * w[0].shape[2]
                dve.wait_ge(w_hi, 2 + n - NCHUNK)
                cut(w[1][:, :, :].rearrange("p k n -> p (k n)"), ring[:, n % RING, 0:size],
                    w[0][:, :, :].rearrange("p k n -> p (k n)")).then_inc(w_lo, 1)

            add_delta(0)
            dve.wait_ge(pe_cond, 3)
            dve.tensor_tensor(mod[:, :, :], PS[:, M1, 0:8 * B].rearrange("p (c b) -> p c b", b=B),
                              cols[:, C_BC:C_BC + 8 * B].rearrange("p (c b) -> p c b", b=B), ALU.add).then_inc(dve_cond, 1)
            dve.wait_ge(pe_cond, 4)
            dve.wait_ge(ld_wc, 32)
            dve.tensor_tensor(a_sb[:, :], PS[0:B, VAL, :], a_sb[:, :], ALU.add).then_inc(dve_cond, 1)
            add_delta(1)
            dve.wait_ge(w_hi, 1)
            cut(wqkv[1][:, :, :], wqkv_f, wqkv[0][:, :, :]).then_inc(w_lo, 1)
            dve.wait_ge(dve_cond, 2)
            dve.tensor_copy(par[:, :, T_G1:T_G1 + 2].rearrange("p b c -> p c b"), mod[:, 0:2, :])
            dve.tensor_copy(par[:, :, T_G2:T_G2 + 2].rearrange("p b c -> p c b"), mod[:, 4:6, :])
            dve.wait_ge(pe_cond, 5)
            dve.tensor_tensor(par[:, :, T_QB:T_QB + 6].rearrange("p b c -> p c b"),
                              PS[:, M1, 0:6 * B].rearrange("p (c b) -> p c b", b=B),
                              cols[:, C_BQKV:C_BQKV + 6 * B].rearrange("p (c b) -> p c b", b=B), ALU.add).then_inc(dve_cond, 1)
            dve.wait_ge(dve_cond, 4)
            parameters_a(0)
            add_delta(2)
            for i in range(2):
                last = dve.memset(v_aug[i][:, :, :, DH:32], 1.0)
            last.then_inc(init_done, 1)
            add_delta(3)
            dve.wait_ge(delta_ready, 4)
            adapter_down(0)
            for n in range(4, NCHUNK // 2):
                add_delta(n)
                if n == 6:
                    adapter_down(1)
            x1_sum(0, 0, X)
            stats1(0, 0)
            norm1(0, 0)
            x1_sum(1, 1, Y)
            stats1(1, 1)
            norm1(1, 1)
            q_low(0)
            k_low(0)
            parameters_a(1)
            weights_low(NCHUNK, wf1)
            q_low(1)
            k_low(1)
            dve.wait_ge(pe_cond, 6)
            dve.tensor_tensor(par[:, :, T_F1:T_F1 + FT].rearrange("p b c -> p c b"),
                              PS[:, VAL, 0:FT * B].rearrange("p (c b) -> p c b", b=B),
                              cols[:, C_BF1:C_BF1 + FT * B].rearrange("p (c b) -> p c b", b=B), ALU.add).then_inc(dve_cond, 1)
            weights_low(NCHUNK + 1, wf2)
            weights_low(NCHUNK + 2, wo)
            for n in range(SM_STEPS):
                row_max(0, n)
            adapter_down(2)
            parameters_a(2)
            dve.wait_ge(dve_cond, 5)
            phase2(0, 0)
            phase1(1, 1)
            phase2(1, 1)
            with dve.Fori(2, B - 3, 2) as j:
                for u in range(2):
                    phase1(j + u, u)
                    phase2(j + u, u)
            for i in range(B - 2, B + 2):
                phase1(i, i % 2)
                phase2(i, i % 2)

        @block.tensor
        def _(pe):
            def three(out, terms, first=True, last=True, **kw):
                n = len(terms)
                for i, (lhs, rhs) in enumerate(terms):
                    for a, c in ((0, 0), (0, 1), (1, 0)):
                        m = pe.matmul(out, lhs[a], rhs[c], start=first and i == 0 and a == c == 0,
                                      stop=last and i == n - 1 and a == 1, **kw)
                return m

            def pair(x, *at):
                return [p[at] for p in x]

            full = slice(None)

            def down(b, at):
                pe.wait_ge(ld_xT, nth(b, 16, 16))
                pe.wait_ge(wd_ready, nth(b, 1, 1))
                for k in range(KT):
                    m = pe.matmul(PS[:, at, 0:P], wd_cur[:, k, :], xT[:, k, :], start=k == 0, stop=k == KT - 1)
                m.then_inc(down_done, 1)

            def up(b, at):
                pe.wait_ge(relu_ready, nth(b, 1, 1))
                for t in range(TT):
                    m = pe.matmul(PS[:, at, t * D:(t + 1) * D], downT[:, t * 128:(t + 1) * 128],
                                  w_ad[:, bass.ds(b, 1), D:2 * D].rearrange("p o n -> p (o n)"), start=True, stop=True)
                m.then_inc(up_done, 1)

            def transpose4(out, x):
                for f in range(KT):
                    for t in range(TT):
                        m = pe.transpose(out[:, f * P + t * 128:f * P + (t + 1) * 128], x[:, t, f * 128:(f + 1) * 128],
                                         ident[:, :])
                return m

            def h1_transpose(b, at):
                pe.wait_ge(h1_ready, nth(b, 1, 1))
                transpose4(bank(at), h1).then_inc(h1tr_done, 1)

            def h2_transpose(a):
                pe.wait_ge(h2_ready, nth(a, 1, 1))
                transpose4(bank(Y), h2).then_inc(h2tr_done, 1)

            def project_tile(w, at, g):
                c = slice((w * G + g) * 128, (w * G + g + 1) * 128)
                return three(PS[:, at, g * P:(g + 1) * P],
                             [(pair(wqkv, full, k, c), pair(h1T, full, k, full)) for k in range(KT)])

            def project_q():
                project_tile(0, B_Q, 0)
                project_tile(0, B_Q, 1).then_inc(q_done, 1)

            def project_k(between=None):
                project_tile(1, B_K, 0)
                if between is not None:
                    o_transpose(between)
                project_tile(1, B_K, 1).then_inc(k_done, 1)

            def project_v():
                for t in range(TT):
                    c = slice(t * 128, (t + 1) * 128)
                    m = three(PS[:, B_V, t * D:(t + 1) * D],
                              [(pair(h1T, full, k, c), pair(wqkv, full, k, slice(2 * D, 3 * D))) for k in range(KT)])
                m.then_inc(v_done, 1)

            def negmax_transpose(i):
                pe.wait_ge(sm_read, nth(i, SM_STEPS, SM_STEPS))
                for t in range(TT):
                    m = pe.transpose(PS[0:NH, X, t * 128:(t + 1) * 128], negmax[:, t, :], ident[:, :])
                m.then_inc(mtr_done, 1)

            def o_transpose(a):
                pe.wait_ge(o_copied, nth(a, 2, 2))
                for t in range(TT):
                    for s in range(SET):
                        m = pe.transpose(PS[:, M0 + t, s * 128:(s + 1) * 128], o_aug[:, s, t * 128:(t + 1) * 128],
                                         ident[:, :])
                m.then_inc(otr_done, 1)

            def o_back(a):
                pe.wait_ge(o_ready, nth(a, 1, 1))
                transpose4(bank(M0), o_tok).then_inc(ontr_done, 1)

            def project_o(a):
                pe.wait_ge(oT_hi, nth(a, 1, 1))
                pe.wait_ge(oT_lo, nth(a, 1, 1))
                for t in range(TT):
                    c = slice(t * 128, (t + 1) * 128)
                    m = three(PS[:, M1, t * D:(t + 1) * D],
                              [(pair(oT, full, k, c), pair(wo, full, k, full)) for k in range(KT)])
                m.then_inc(wo_done, 1)

            def mlp_in(c, m4):
                if m4 == 0:
                    pe.wait_ge(h2T_hi, nth(c, 1, 1))
                    pe.wait_ge(h2T_lo, nth(c, 1, 1))
                elif m4 >= 2:
                    pe.wait_ge(gelu_done, nth(c, 4, m4 - 1))
                for f in range(2):
                    col = slice((2 * m4 + f) * 128, (2 * m4 + f + 1) * 128)
                    m = three(PS[:, F1_BANKS[m4], f * P:(f + 1) * P],
                              [(pair(wf1, full, k, col), pair(h2T, full, k, full)) for k in range(KT)])
                m.then_inc(f1_done, 1)

            def mlp_out(c):
                for k in range(FT):
                    if k % 2 == 0:
                        pe.wait_ge(g_lo_done, nth(c, 4, k // 2 + 1))
                    for t in range(TT):
                        col = slice(t * 128, (t + 1) * 128)
                        m = three(PS[:, VAL, t * D:(t + 1) * D],
                                  [(pair((g_hi, g_lo), full, k, col), pair(wf2, full, k, full))],
                                  first=k == 0 and t == 0, last=k == FT - 1, skip_group_check=True)
                m.then_inc(f2_done, 1)

            def max_step(b, par_, n):
                s, t, j = n // 4, n // 2 % 2, 2 * (n % 2)
                g, half = s // HALF, s % HALF
                if n == 0:
                    pe.wait_ge(q_stacked, nth(b, STACK_DMAS * 16, STACK_DMAS * 16))
                    pe.wait_ge(k_stacked, nth(b, STACK_DMAS * 16, STACK_DMAS * 16))
                if n == 1 and later(b, 2):
                    pe.wait_ge(a1o_ready, nth(b - 2, 1, 1))
                if n >= 2:
                    pe.wait_ge(sm_read, nth(b, SM_STEPS, n - 1))
                for p in range(2):
                    m = pe.matmul(PS[:, M0 + n % 2, p * P:(p + 1) * P],
                                  q_stack[par_][0:MROW, half, j + p, g, t * 128:(t + 1) * 128],
                                  k_stack[par_][0:MROW, j + p, g, :], start=True, stop=True)
                m.then_inc(sm_done, 1)

            def score_step(b, par_, n):
                s, j = n // SET_STEPS, n % SET_STEPS
                g, half = s // HALF, s % HALF
                if n >= S_BANKS:
                    pe.wait_ge(exp_done, nth(b, ST_STEPS, n - S_BANKS + 1))
                for t in range(TT):
                    m = pe.matmul(PS[:, n % S_BANKS, t * P:(t + 1) * P],
                                  k_stack[par_][0:MROW + 1, j, g, t * 128:(t + 1) * 128],
                                  q_stack[par_][0:MROW + 1, half, j, g, :], start=True, stop=True)
                m.then_inc(st_done, 1)

            def values(b, par_, s, t):
                if t == 0:
                    pe.wait_ge(exp_done, nth(b, ST_STEPS, SET_STEPS * (s + 1)))
                    if s == 2:
                        pe.wait_ge(o_copied, nth(b, 2, 1))
                for j in range(PP):
                    m = pe.matmul(PS[32 * j:32 * j + 32, VAL, s % 2 * P:(s % 2 + 1) * P],
                                  v_aug[par_][:, t, s * PP + j, :], probs[s % 2][:, j, t, :],
                                  start=t == 0, stop=t == TT - 1)
                if t == TT - 1:
                    m.then_inc(pv_done, 1)

            def phase1(i, par_):
                b, a, c = i + 1, i - 1, i - 2
                if real(b):
                    pe.wait_ge(h1T_hi, nth(b, 1, 1))
                    pe.wait_ge(h1T_lo, nth(b, 1, 1))
                    pe.wait_ge(exp_done, nth(a, ST_STEPS, ST_STEPS - 2))
                    project_q()
                if real(a):
                    values(a, 1 - par_, SET - 1, 0)
                    values(a, 1 - par_, SET - 1, 1)
                if real(i):
                    negmax_transpose(i)
                if real(b):
                    project_k(between=a)
                    project_v()
                elif real(a):
                    o_transpose(a)
                if real(a):
                    o_back(a)
                if real(c):
                    mlp_in(c, 0)
                if real(c):
                    if real(i):
                        pe.wait_ge(negmaxT_ready, nth(i, 1, 1))
                    mlp_in(c, 1)
                if real(a):
                    project_o(a)
                if real(c):
                    mlp_in(c, 2)
                    mlp_in(c, 3)
                    mlp_out(c)

            def phase2(i, par_):
                a, c = i - 1, i - 2
                if not real(i):
                    if real(a):
                        h2_transpose(a)
                        pe.wait_ge(a2y_ready, nth(c, 1, 1))
                    return
                if real(i + 1):
                    pe.wait_ge(q_lo, nth(i + 1, 1, 1))
                    pe.wait_ge(k_lo, nth(i + 1, 1, 1))
                    pe.wait_ge(v_ready, nth(i + 1, 1, 1))
                pe.wait_ge(m_stacked, nth(i, 16, 16))
                for n in range(ST_STEPS):
                    score_step(i, par_, n)
                    if n == 0 and real(i + 2):
                        down(i + 2, X)
                    if real(i + 1):
                        max_step(i + 1, 1 - par_, n)
                    if n == 2 and real(a):
                        h2_transpose(a)
                    if n == 3 and real(i + 2):
                        up(i + 2, X)
                    if n == 9 and real(i + 2):
                        h1_transpose(i + 2, X)
                    s, t = (n - 5) // SET_STEPS, (n - 5) % SET_STEPS
                    if n >= 5 and t < TT:
                        if n == 5 and real(c):
                            pe.wait_ge(a2y_ready, nth(c, 1, 1))
                        values(i, par_, s, t)

            def delta_chunk(n):
                b2, half = n // 2, n % 2
                pe.wait_ge(ld_ring[n % RING], 16 * (n // RING + 1))
                if half == 0 and b2 >= 2:
                    pe.wait_ge(delta_copied, b2 - 1)
                data = ring[:, n % RING, :].rearrange("p (k j n) -> p k j n", k=KH, j=2)
                for k in range(KH):
                    for j in range(2):
                        at = 32 * (2 * half + j)
                        m = pe.matmul(PS[at:at + 32, b2 % 2, :], hbd[:, k, :], data[:, k, j, :],
                                      start=k == 0, stop=k == KH - 1)
                m.then_inc(delta_done, 1)

            def delta_transpose(n):
                pe.wait_ge(delta_copied, n + 1)
                if n >= 2:
                    pe.wait_ge(delta_ready, n - 1)
                for c in range(4):
                    m = pe.transpose(PS[:, 2 + n % 2, c * 128:(c + 1) * 128], dtmp[:, n % 2, c * 128:(c + 1) * 128],
                                     ident[:, :])
                m.then_inc(deltaT_done, 1)

            def columns(at, tiles, w, x):
                for c in range(tiles):
                    for k in range(KT):
                        m = pe.matmul(PS[:, at, c * B:(c + 1) * B], w[:, k, c * 128:(c + 1) * 128],
                                      x[:, k, :], start=k == 0, stop=k == KT - 1)
                return m

            pe.wait_ge(ld_const, 16 * 4)
            pe.wait_ge(ld_small, 16)
            for f in range(KT):
                m = pe.matmul(PS[:, M1, f * B:(f + 1) * B], wt1[:, f * 128:(f + 1) * 128], cond_t, start=True, stop=True)
            m.then_inc(pe_cond, 1)
            delta_chunk(0)
            pe.wait_ge(act_cond, 1)
            columns(VAL, KT, wt2, s1).then_inc(pe_cond, 1)
            delta_chunk(1)
            delta_transpose(0)
            delta_chunk(2)
            pe.wait_ge(act_cond, 2)
            pe.wait_ge(ld_wc, 32)
            columns(M1, 8, wc, s2).then_inc(pe_cond, 1)
            for k in range(KT):
                m = pe.matmul(PS[0:B, VAL, :], s2[:, k, :], wc[:, k, 4 * D:6 * D], start=k == 0, stop=k == KT - 1)
            m.then_inc(pe_cond, 1)
            delta_chunk(3)
            delta_transpose(1)
            delta_chunk(4)
            pe.wait_ge(ld_wqkv, 16)
            pe.wait_ge(dve_cond, 2)
            columns(M1, 6, wqkv_f, mod[:, 2:4, :]).then_inc(pe_cond, 1)
            delta_chunk(5)
            for n in range(3, NCHUNK // 2):
                delta_transpose(n - 1)
                delta_chunk(2 * n)
                delta_chunk(2 * n + 1)
                if n == 5:
                    down(0, X)
                if n == 7:
                    down(1, Y)
            delta_transpose(NCHUNK // 2 - 1)
            pe.wait_ge(delta_ready, NCHUNK // 2)
            up(0, X)
            up(1, Y)
            h1_transpose(0, X)
            pe.wait_ge(h1T_hi, 1)
            pe.wait_ge(h1T_lo, 1)
            pe.wait_ge(w_lo, 1)
            project_q()
            project_k()
            project_v()
            h1_transpose(1, Y)
            pe.wait_ge(ld_ring[NCHUNK % RING], 16 * (NCHUNK // RING + 1))
            pe.wait_ge(dve_cond, 3)
            columns(VAL, 8, wf1_f, mod[:, 6:8, :]).then_inc(pe_cond, 1)
            pe.wait_ge(h1T_hi, 2)
            pe.wait_ge(h1T_lo, 2)
            pe.wait_ge(q_lo, 1)
            pe.wait_ge(k_lo, 1)
            pe.wait_ge(v_ready, 1)
            project_q()
            project_k()
            project_v()
            for n in range(SM_STEPS):
                max_step(0, 0, n)
            negmax_transpose(0)
            pe.wait_ge(ones_set, 2)
            pe.wait_ge(dve_cond, 5)
            phase2(0, 0)
            pe.wait_ge(w_lo, 4)
            phase1(1, 1)
            phase2(1, 1)
            with pe.Fori(2, B - 3, 2) as j:
                for u in range(2):
                    phase1(j + u, u)
                    phase2(j + u, u)
            for i in range(B - 2, B + 2):
                phase1(i, i % 2)
                phase2(i, i % 2)


def kernel(x, cond_256, fside_BxS_0, L0_cond_Wd, L0_cond_bd, L0_cond_Wu, L0_cond_bu, L0_cond_Wdd, L0_cond_bdd,
           L0_cond_Wdu, L0_cond_bdu, L1_cond_W_t1, L1_cond_b_t1, L1_cond_W_t2, L1_cond_b_t2, L1_cond_W_c,
           L1_cond_b_c, L1_cond_W_qkv, L1_cond_b_qkv, L1_cond_W_o, L1_cond_b_o, L1_cond_W_f1, L1_cond_b_f1,
           L1_cond_W_f2, L1_cond_b_f2):
    import numpy as np
    import concourse.bacc as bacc
    from concourse.bass_utils import run_bass_kernel_spmd as run

    (x, h, c, Wd, bd, Wu, bu, Wdd, bdd, Wdu, bdu, Wt1, bt1, Wt2, bt2, Wc, bc, Wqkv, bqkv, Wo, bo, Wf1, bf1, Wf2,
     bf2) = (np.asarray(a) for a in (
         x, cond_256, fside_BxS_0, L0_cond_Wd, L0_cond_bd, L0_cond_Wu, L0_cond_bu, L0_cond_Wdd, L0_cond_bdd,
         L0_cond_Wdu, L0_cond_bdu, L1_cond_W_t1, L1_cond_b_t1, L1_cond_W_t2, L1_cond_b_t2, L1_cond_W_c,
         L1_cond_b_c, L1_cond_W_qkv, L1_cond_b_qkv, L1_cond_W_o, L1_cond_b_o, L1_cond_W_f1, L1_cond_b_f1,
         L1_cond_W_f2, L1_cond_b_f2))

    def by_tile(w):
        return w.reshape(-1, 128, w.shape[1]).transpose(1, 0, 2)

    def column(v, repeat=1):
        return np.repeat(v.reshape(-1, 128).T, repeat, axis=1)

    cols = np.concatenate([column(bd), column(bt1), column(bt2), by_tile(c.T).reshape(128, -1),
                           column(bc[:4 * D], B), column(bqkv, B), column(bf1, B)], axis=1)
    hbd = np.zeros((4, 32, KH, 4, B), h.dtype)
    for j in range(4):
        hbd[j, :, :, j, :] = h.T.reshape(KH, 32, B).transpose(1, 0, 2)
    small = np.zeros((128, 768 + B), h.dtype)
    small[:HC, 0:256] = Wt1.T
    small[:, 256:768] = by_tile(Wt2.T).reshape(128, -1)
    small[:HC, 768:] = h.T
    def down_columns(w):
        return w.reshape(BN, KT, 128, -1).transpose(2, 1, 0, 3).reshape(128, 2 * 128, -1)

    def up_columns(w):
        return w.reshape(D, BN, -1).transpose(1, 0, 2)
    base = np.concatenate([f(w)[:, :, 0] for w_ in ((Wd, Wu), (bdd, bdu)) for f, w in zip((down_columns, up_columns), w_)],
                          axis=1)
    gen = np.concatenate([down_columns(Wdd), up_columns(Wdu)], axis=1)
    gen = gen.reshape(128, 8, 4, 2, 2, 4, KH, 32).transpose(1, 3, 5, 7, 6, 4, 2, 0).reshape(NCHUNK, 128, CHUNK)

    arrays = {
        "x_tok": x, "x_feat": x.transpose(0, 2, 1), "cols_in": cols, "hbd_in": hbd.reshape(128, KH, 32),
        "ident_in": np.eye(128, dtype=np.float32), "base_in": base, "small_w": small, "wc_in": by_tile(Wc.T),
        "wqkv_in": by_tile(Wqkv.T), "wf1_in": by_tile(Wf1.T).reshape(128, -1), "wdelta_in": gen,
        "wf2_in": by_tile(Wf2.T).reshape(128, -1), "wo_in": by_tile(Wo.T).reshape(128, -1),
        "rows_in": np.broadcast_to(np.stack([bu, bo, bf2]), (128, 3, D)),
        "bcrow_in": np.broadcast_to(bc[4 * D:], (B, 2 * D)),
    }
    arrays = {k: np.ascontiguousarray(v) for k, v in arrays.items()}
    nc = bacc.Bacc("TRN2", target_bir_lowering=False, num_devices=1)
    args = {k: nc.dram_tensor(k, v.shape, mybir.dt.from_np(v.dtype), kind="ExternalInput").ap()
            for k, v in arrays.items()}
    args["out"] = nc.dram_tensor("out", (B, P, D), FP32, kind="ExternalOutput").ap()
    build(nc, **args)
    r = run(nc, [arrays], core_ids=[0])
    return r.results[0]["out"]
```

```python
import concourse.bass as bass
from concourse import mybir
from contextlib import ExitStack

FP32 = mybir.dt.float32
F32R = mybir.dt.float32r
ALU = mybir.AluOpType
ACT = mybir.ActivationFunctionType
AX = mybir.AxisListType

B = 8
P = 256
D = 256
BN = 128
HC = 64
NH, DH = 16, 16
F = 1024
KT = D // 128
TT = P // 128
FT = F // 128
EPS = 1e-5
DELTA_SCALE = 0.1

G, HALF, PP = 2, 2, 4
SET = G * HALF
STK = 3 * DH
MROW = 2 * STK
STACK_DMAS = HALF
STACK_PARTS = ((0, 1, 2), (0, 2, 1))

KH = 2
NCHUNK = 16
CHUNK = 2048
RING = 3

C_BD, C_BT1, C_BT2, C_EMB = 0, 1, 3, 5
C_BC = C_EMB + KT * B
C_BQKV = C_BC + 8 * B
C_BF1 = C_BQKV + 6 * B
C_END = C_BF1 + FT * B

T_G1, T_QB, T_KB, T_VB, T_G2, T_F1 = 0, 2, 4, 6, 8, 10
NPAR = 18
NPAR_A = 6

SM_STEPS = NH // 2 * TT
ST_STEPS = NH
SET_STEPS = ST_STEPS // SET
AHEAD = 2
H2_AT, H2T_AT = 3, 7

S_BANKS = 3
B_Q, B_K, B_V = 1, 2, 0
B_F = B_Q
M0, M1 = 3, 4
VAL = 5
X, Y = 6, 7
F1_BANKS = (Y, X, Y, X)
MAX_BANKS = (M0, M1)
MAX_BANKS_0 = (M0, M1, X, Y)


def build(nc, x_tok, x_feat, cols_in, hbd_in, ident_in, base_in, small_w, wc_in, wqkv_in, wf1_in, wdelta_in,
          wf2_in, wo_in, rows_in, bcrow_in, out):
    ctx = ExitStack()
    with ctx:
        def sb(name, shape, dt=FP32):
            return ctx.enter_context(nc.sbuf_tensor(name, shape, dt))

        def sem(name):
            return ctx.enter_context(nc.semaphore(name))

        wqkv = [sb(f"wqkv_{p}", [128, KT, 3 * D], F32R) for p in ("hi", "lo")]
        wo = [sb(f"wo_{p}", [128, KT, D], F32R) for p in ("hi", "lo")]
        wf1 = [sb(f"wf1_{p}", [128, KT, F], F32R) for p in ("hi", "lo")]
        wf2 = [sb(f"wf2_{p}", [128, FT, D], F32R) for p in ("hi", "lo")]
        k_stack = [sb(f"k_stack{i}", [128, PP, G, P], F32R) for i in range(2)]
        q_stack = [sb(f"q_stack{i}", [128, HALF, PP, G, P], F32R) for i in range(2)]
        ring = sb("ring", [128, RING, CHUNK])
        probs = [ring[:, i, :].rearrange("p (j t q) -> p j t q", j=PP, t=TT) for i in range(2)]
        gelu_f = ring[:, 0, :].rearrange("p (f n) -> p f n", f=FT)
        a2y, h2T_f = [ring[:, 2, i * 512:(i + 1) * 512].rearrange("p (k n) -> p k n", k=KT) for i in (2, 3)]
        x2 = [ring[:, 2, i * 512:(i + 1) * 512].rearrange("p (t n) -> p t n", t=TT) for i in range(2)]
        g_hi = sb("g_hi", [128, FT, P], F32R)
        g_lo = sb("g_lo", [128, FT, P], F32R)
        qk_parts = g_hi[:, :, :].rearrange("p (w h g) n -> p w h g n", w=2, h=2)
        arena = sb("arena", [128, 6656])
        wc = arena[:, 0:3072].rearrange("p (k n) -> p k n", k=KT)
        wqkv_f = arena[:, 3072:4608].rearrange("p (k n) -> p k n", k=KT)
        wt1 = arena[0:HC, 4608:4864]
        wt2 = arena[:, 4864:5376].rearrange("p (k n) -> p k n", k=KT)
        cond_t = arena[0:HC, 5376:5376 + B]
        wf1_f = ring[:, NCHUNK % RING, :].rearrange("p (k n) -> p k n", k=KT)

        def tile(at):
            return arena[:, at:at + 512].rearrange("p (t n) -> p t n", t=2)
        x_in = [tile(0), tile(512)]
        h1T_f = tile(1024)
        xT = tile(1536)
        h1 = tile(2048)
        h2 = tile(2560)
        o_tok = tile(3072)
        a12 = [tile(3584), tile(4096)]
        v_aug = [arena[:, 4608 + i * 1024:5632 + i * 1024].rearrange("p (t h n) -> p t h n", t=TT, h=NH)
                 for i in range(2)]
        o_aug = sb("o_aug", [128, SET, P])
        dtmp = o_aug[:, :, :].rearrange("p (i s) n -> p i (s n)", i=2)
        w_ad = sb("w_ad", [128, B, 2 * D])
        base = sb("base", [128, 1024])
        downT = base[:, 512:768]
        wd_cur = base[:, 768:1024].rearrange("p (k n) -> p k n", k=KT)
        a1bo = base[:, 0:256]
        a2bf2 = base[:, 256:512]
        h1T = [sb(f"h1T_{p}", [128, KT, P], F32R) for p in ("hi", "lo")]
        h2T = [sb(f"h2T_{p}", [128, KT, P], F32R) for p in ("hi", "lo")]
        oT = [sb(f"oT_{p}", [128, KT, P], F32R) for p in ("hi", "lo")]
        ident = sb("ident", [128, 128])
        hbd = sb("hbd", [128, KH, 32])
        cols = sb("cols", [128, C_END])
        rows = sb("rows", [128, 3, D])
        par = sb("par", [128, B, NPAR])
        par_a = sb("par_a", [128, NPAR_A])
        par_t = [sb(f"par_t{i}", [128, NPAR - NPAR_A]) for i in range(2)]
        s1 = sb("s1", [128, KT, B])
        z2 = sb("z2", [128, KT, B])
        s2 = sb("s2", [128, KT, B])
        mod = sb("mod", [128, 8, B])
        negmax = sb("negmax", [128, TT, NH])
        negmaxT = sb("negmaxT", [NH, P], F32R)
        rden = sb("rden", [128, TT, NH])
        neghalf = sb("neghalf", [128, TT])
        eps = sb("eps", [128, TT])
        bn1 = sb("bn1", [128, TT, 6])
        bn2 = sb("bn2", [128, TT, 6])
        mv1 = sb("mv1", [128, TT, 2])
        mv2 = sb("mv2", [128, TT, 2])
        ve1 = sb("ve1", [128, TT])
        ve2 = sb("ve2", [128, TT])
        rs1 = sb("rs1", [128, TT])
        rs2 = sb("rs2", [128, TT])
        a_sb = sb("a_sb", [B, 2 * D])
        scrap = sb("scrap", [128, 2])

        PS = ctx.enter_context(nc.psum_tensor("PS", [128, 8, 512], FP32))

        def bank(n):
            return PS[:, n, :]

        qk_scr = nc.dram_tensor("qk_scr", (2, HALF * PP, 3, DH, G * P), FP32).ap()
        a_scr = nc.dram_tensor("a_scr", (B, 2 * D), FP32).ap()
        x1_scr = nc.dram_tensor("x1_scr", (B, P, D), FP32).ap()

        (ld_const, ld_small, ld_wc, ld_wqkv, ld_x, ld_xT, ld_a12, stored, a_saved) = map(sem, (
            "ld_const", "ld_small", "ld_wc", "ld_wqkv", "ld_x", "ld_xT", "ld_a12", "stored", "a_saved"))
        (ld_rows, ld_x2, x1_saved, h1T_f_ready, h2T_f_ready) = map(sem, (
            "ld_rows", "ld_x2", "x1_saved", "h1T_f_ready", "h2T_f_ready"))
        ld_ring = [sem(f"ld_ring{i}") for i in range(RING)]
        (delta_done, delta_copied, deltaT_done, delta_ready) = map(sem, (
            "delta_done", "delta_copied", "deltaT_done", "delta_ready"))
        (pe_cond, act_cond, dve_cond, w_hi, w_lo, init_done, pool_init, ones_set) = map(sem, (
            "pe_cond", "act_cond", "dve_cond", "w_hi", "w_lo", "init_done", "pool_init",
            "ones_set"))
        (xb_ready, wd_ready, pa_ready, pt_ready, down_done, relu_ready, up_done, x1_ready, st1_ready, rs1_ready,
         h1_ready, h1tr_done, h1T_hi, h1T_lo, q_done, q_hi, q_lo, k_done, k_hi, k_lo, v_done, v_ready) = map(sem, (
            "xb_ready", "wd_ready", "pa_ready", "pt_ready", "down_done", "relu_ready", "up_done", "x1_ready",
            "st1_ready", "rs1_ready", "h1_ready", "h1tr_done", "h1T_hi", "h1T_lo", "q_done", "q_hi", "q_lo",
            "k_done", "k_hi", "k_lo", "v_done", "v_ready"))
        (q_saved, k_saved, q_stacked, k_stacked, sm_done, sm_read, mtr_done, negmaxT_ready, m_stacked, st_done,
         exp_done, pv_done, o_copied, otr_done, rden_ready, o_ready, ontr_done, oT_hi, oT_lo, wo_done) = map(sem, (
            "q_saved", "k_saved", "q_stacked", "k_stacked", "sm_done", "sm_read", "mtr_done", "negmaxT_ready",
            "m_stacked", "st_done", "exp_done", "pv_done", "o_copied", "otr_done", "rden_ready", "o_ready",
            "ontr_done", "oT_hi", "oT_lo", "wo_done"))
        (abias_ready, x2base_ready, a1o_ready, x2_ready, st2_ready, rs2_ready, h2_ready, x2b_ready, h2tr_done, h2T_hi,
         h2T_lo, f1_done, gelu_done, g_hi_done, g_lo_done, f2_done, a2y_ready, x3_ready, ve1_ready, ve2_ready,
         bns1_ready, bns2_ready) = map(sem, (
            "abias_ready", "x2base_ready", "a1o_ready", "x2_ready", "st2_ready", "rs2_ready", "h2_ready", "x2b_ready",
            "h2tr_done", "h2T_hi", "h2T_lo", "f1_done", "gelu_done", "g_hi_done", "g_lo_done", "f2_done",
            "a2y_ready", "x3_ready", "ve1_ready", "ve2_ready",
            "bns1_ready", "bns2_ready"))

        def nth(b, n, k):
            return b * n + k

        def real(b):
            return not isinstance(b, int) or 0 <= b < B

        def later(b, n=1):
            return not isinstance(b, int) or b >= n

        def bare(i):
            return isinstance(i, int) and i == 1

        def final(b):
            return isinstance(b, int) and b == B - 1

        def each_tile(b):
            return b.unsqueeze(1).to_broadcast([128, TT, D])

        def g2_column(par_, f):
            return par_t[par_][:, T_G2 - NPAR_A + f:T_G2 - NPAR_A + f + 1]

        def vb_column(par_, f):
            return par_t[par_][:, T_VB - NPAR_A + f:T_VB - NPAR_A + f + 1]

        block = ctx.enter_context(nc.Block())

        @block.sync
        def _(sp):
            def load_chunk(n):
                if n >= RING:
                    sp.wait_ge(delta_done, n - RING + 1)
                src = wdelta_in[n] if n < NCHUNK else (wf1_in, wf2_in, wo_in)[n - NCHUNK]
                sp.dma_start(ring[:, n % RING, 0:src.shape[1]], src).then_inc(ld_ring[n % RING], 16)

            def load_front(b, par_):
                if later(b):
                    sp.wait_ge(down_done, nth(b, 1, 0))
                sp.dma_start(xT, x_feat[bass.ds(b, 1)].rearrange("o (k p) n -> p (o k) n", p=128)).then_inc(ld_xT, 16)
                if later(b, 2):
                    sp.wait_ge(x1_saved, nth(b, 16, 0))
                    sp.wait_ge(h1_ready, nth(b, 1, 0))
                sp.dma_start(x_in[par_], x_tok[bass.ds(b, 1)].rearrange("o (t p) n -> p (o t) n", p=128))\
                  .then_inc(ld_x, 16)

            def save_x1(b, par_):
                sp.wait_ge(x1_ready, nth(b, 1, 1))
                sp.dma_start(x1_scr[bass.ds(b, 1)].rearrange("o (t p) n -> p (o t) n", p=128), x_in[par_])\
                  .then_inc(x1_saved, 16)

            def store(b, par_):
                sp.wait_ge(x3_ready, nth(b, 1, 1))
                sp.dma_start(out[bass.ds(b, 1)].rearrange("o (t p) n -> p (o t) n", p=128), x2[par_])\
                  .then_inc(stored, 16)

            def load_residual(b, par_):
                if later(b, 2):
                    sp.wait_ge(stored, nth(b - 1, 16, 0))
                if later(b):
                    sp.wait_ge(x2base_ready, nth(b, 1, 0))
                if not real(b + 2):
                    sp.wait_ge(x1_saved, nth(b, 16, 16))
                sp.dma_start(x2[par_], x1_scr[bass.ds(b, 1)].rearrange("o (t p) n -> p (o t) n", p=128))\
                  .then_inc(ld_x2, 16)
                sp.dma_start(a12[par_].rearrange("p t n -> p (t n)"),
                             a_scr[bass.ds(b, 1), :].to_broadcast([128, 2 * D])).then_inc(ld_a12, 16)

            def save_qk(b, w, hi, lo, saved, stacked):
                if later(b):
                    sp.wait_ge(stacked, nth(b, STACK_DMAS * 16, 0))
                first, second, last = STACK_PARTS[w]
                sp.wait_ge(hi, nth(b, 1, 1))
                for part in (first, second):
                    sp.dma_start(qk_scr[w, :, part], qk_parts[:, w, 0].rearrange("p g n -> p (g n)").bitcast(FP32))\
                      .then_inc(saved, 16)
                sp.wait_ge(lo, nth(b, 1, 1))
                sp.dma_start(qk_scr[w, :, last], qk_parts[:, w, 1].rearrange("p g n -> p (g n)").bitcast(FP32))\
                  .then_inc(saved, 16)

            def stack(b, w, dst, saved, done):
                sp.wait_ge(saved, nth(b, 48, 48))
                for half in range(HALF):
                    at = half * STK
                    to = dst[at:at + STK, half] if w == 0 else dst[at:at + STK]
                    sp.dma_start(to.rearrange("r j g n -> r j (g n)").bitcast(FP32),
                                 qk_scr[w, half * PP:(half + 1) * PP].rearrange("j part d n -> (part d) j n"))\
                      .then_inc(done, 16)

            def stack_negmax(b, par_):
                sp.wait_ge(negmaxT_ready, nth(b, 1, 1))
                sp.dma_start(q_stack[par_][MROW:MROW + 1].rearrange("o a j g n -> o (a j g) n").bitcast(FP32),
                             negmaxT[:, :].bitcast(FP32)).then_inc(m_stacked, 16)

            def phase1(i, par_):
                if real(i + 2):
                    load_front(i + 2, par_)
                if real(i + 1):
                    save_qk(i + 1, 0, q_hi, q_lo, q_saved, q_stacked)
                if real(i):
                    stack_negmax(i, par_)
                if real(i + 1):
                    save_qk(i + 1, 1, k_hi, k_lo, k_saved, k_stacked)
                    stack(i + 1, 0, q_stack[1 - par_], q_saved, q_stacked)
                    stack(i + 1, 1, k_stack[1 - par_], k_saved, k_stacked)

            def phase2(i, par_):
                if real(i - 2):
                    store(i - 2, par_)
                if real(i):
                    load_residual(i, par_)
                if real(i + 2):
                    save_x1(i + 2, par_)

            sp.dma_start(cols[:, :], cols_in).then_inc(ld_const, 16)
            sp.dma_start(hbd[:, :, :], hbd_in).then_inc(ld_const, 16)
            sp.dma_start(arena[:, 4608:5376 + B], small_w).then_inc(ld_small, 16)
            load_chunk(0)
            sp.dma_start(base[:, :], base_in).then_inc(ld_const, 16)
            sp.dma_start(ident[:, :], ident_in).then_inc(ld_const, 16)
            load_chunk(1)
            sp.dma_start(wc, wc_in).then_inc(ld_wc, 16)
            sp.dma_start(a_sb[:, :], bcrow_in).then_inc(ld_wc, 16)
            load_chunk(2)
            sp.dma_start(wqkv_f, wqkv_in).then_inc(ld_wqkv, 16)
            for n in range(3, NCHUNK):
                load_chunk(n)
                if n == 9:
                    sp.wait_ge(pe_cond, 4)
                    load_front(0, 0)
            sp.dma_start(rows[:, :, :], rows_in).then_inc(ld_rows, 16)
            load_front(1, 1)
            for n in range(NCHUNK, NCHUNK + 3):
                load_chunk(n)
            sp.wait_ge(dve_cond, 3)
            sp.dma_start(a_scr, a_sb[:, :]).then_inc(a_saved, 16)
            save_x1(0, 0)
            save_x1(1, 1)
            save_qk(0, 0, q_hi, q_lo, q_saved, q_stacked)
            save_qk(0, 1, k_hi, k_lo, k_saved, k_stacked)
            sp.wait_ge(pool_init, 5)
            stack(0, 0, q_stack[0], q_saved, q_stacked)
            stack(0, 1, k_stack[0], k_saved, k_stacked)
            load_front(2, 0)
            save_qk(1, 0, q_hi, q_lo, q_saved, q_stacked)
            save_qk(1, 1, k_hi, k_lo, k_saved, k_stacked)
            stack(1, 0, q_stack[1], q_saved, q_stacked)
            stack(1, 1, k_stack[1], k_saved, k_stacked)
            stack_negmax(0, 0)
            sp.wait_ge(a_saved, 16)
            sp.wait_ge(w_lo, 4)
            phase2(0, 0)
            phase1(1, 1)
            phase2(1, 1)
            with sp.Fori(2, B - 3, 2) as j:
                for u in range(2):
                    phase1(j + u, u)
                    phase2(j + u, u)
            for i in range(B - 2, B + 2):
                phase1(i, i % 2)
                phase2(i, i % 2)
            sp.wait_ge(stored, 16 * B)

        @block.gpsimd
        def _(pool):
            def rstd(b, st_ready, mv, ve, ve_ready, rs, rs_ready):
                pool.wait_ge(st_ready, nth(b, 1, 1))
                pool.tensor_tensor(ve[:, :], mv[:, :, 1], eps[:, :], ALU.add).then_inc(ve_ready, 1)
                pool.wait_ge(ve_ready, nth(b, 1, 1))
                pool.tensor_tensor(rs[:, :], ve[:, :], neghalf[:, :], ALU.pow).then_inc(rs_ready, 1)

            def biased(b, par_):
                pool.wait_ge(ld_x, nth(b, 16, 16))
                pool.tensor_tensor(x_in[par_], x_in[par_], each_tile(rows[:, 0, :]), ALU.add).then_inc(xb_ready, 1)

            def rstd_front(b):
                rstd(b, st1_ready, mv1, ve1, ve1_ready, rs1, rs1_ready)

            def residual(b, par_):
                if later(b):
                    pool.wait_ge(x2b_ready, nth(b, 1, 0))
                pool.wait_ge(ld_a12, nth(b, 16, 16))
                pool.tensor_tensor(a1bo, a12[par_][:, 0, :], rows[:, 1, :], ALU.mult).then_inc(abias_ready, 1)
                pool.tensor_tensor(a2bf2, a12[par_][:, 1, :], rows[:, 2, :], ALU.mult).then_inc(abias_ready, 1)
                pool.wait_ge(ld_x2, nth(b, 16, 16))
                pool.wait_ge(abias_ready, nth(b, 2, 1))
                pool.tensor_tensor(x2[par_], x2[par_], each_tile(a1bo), ALU.add).then_inc(x2base_ready, 1)

            def residual_end(b, par_):
                rstd(b, st2_ready, mv2, ve2, ve2_ready, rs2, rs2_ready)
                pool.wait_ge(h2_ready, nth(b, 1, 1))
                pool.wait_ge(abias_ready, nth(b, 2, 2))
                pool.tensor_tensor(x2[par_], x2[par_], each_tile(a2bf2), ALU.add).then_inc(x2b_ready, 1)

            def mlp_end(c, par_):
                pool.wait_ge(a2y_ready, nth(c, 1, 1))
                pool.wait_ge(x2b_ready, nth(c, 1, 1))
                pool.tensor_tensor(x2[par_], x2[par_], a2y, ALU.add).then_inc(x3_ready, 1)

            def low(n, lo, whole, hi, ready, lo_ready):
                pool.wait_ge(ready, nth(n, 1, 1))
                pool.tensor_tensor(lo[:, :, :], whole, hi[:, :, :].bitcast(FP32), ALU.subtract).then_inc(lo_ready, 1)

            def phase1(i, par_):
                if real(i + 2):
                    biased(i + 2, par_)
                if real(i - 1):
                    residual(i - 1, 1 - par_)
                if real(i + 2):
                    rstd_front(i + 2)
                if real(i - 1):
                    residual_end(i - 1, 1 - par_)
                    if not final(i - 1):
                        low(i - 1, h2T[1], h2T_f, h2T[0], h2T_f_ready, h2T_lo)

            def phase2(i, par_):
                if real(i - 2) and not final(i - 2):
                    mlp_end(i - 2, par_)
                if real(i + 2):
                    low(i, h1T[1], h1T_f, h1T[0], h1T_f_ready, h1T_lo)

            pool.memset(neghalf[:, :], -0.5).then_inc(pool_init, 1)
            pool.memset(scrap[:, :], 0.0).then_inc(pool_init, 1)
            pool.memset(eps[:, :], EPS).then_inc(pool_init, 1)
            for i in range(2):
                pool.memset(q_stack[i][:, :, :, :, :].bitcast(FP32), 0.0).then_inc(pool_init, 1)
            pool.wait_ge(ld_rows, 16)
            pool.wait_ge(pool_init, 5)
            biased(0, 0)
            biased(1, 1)
            rstd_front(0)
            rstd_front(1)
            for n, w in enumerate((wf1, wf2, wo)):
                size = w[0].shape[1] * w[0].shape[2]
                pool.wait_ge(w_hi, 2 + n)
                pool.tensor_tensor(w[1][:, :, :].rearrange("p k n -> p (k n)"), ring[:, (NCHUNK + n) % RING, 0:size],
                                   w[0][:, :, :].rearrange("p k n -> p (k n)").bitcast(FP32), ALU.subtract)\
                    .then_inc(w_lo, 1)
                if n == 0:
                    biased(2, 0)
            rstd_front(2)
            phase2(0, 0)
            phase1(1, 1)
            phase2(1, 1)
            with pool.Fori(2, B - 3, 2) as j:
                for u in range(2):
                    phase1(j + u, u)
                    phase2(j + u, u)
            for i in range(B - 2, B + 2):
                phase1(i, i % 2)
                phase2(i, i % 2)

        @block.scalar
        def _(act):
            def relu(b, at):
                act.wait_ge(down_done, nth(b, 1, 1))
                if isinstance(b, int) and b == 1:
                    act.wait_ge(up_done, 1)
                act.activation(downT, PS[:, at, 0:P], ACT.Relu, bias=cols[:, C_BD:C_BD + 1]).then_inc(relu_ready, 1)

            def tiles(out, at, func, column=None, scale=False):
                for f in range(KT):
                    kw = {} if column is None else {"scale" if scale else "bias": column(f)}
                    last = act.activation(out[:, f, :], PS[:, at, f * P:(f + 1) * P], func, **kw)
                return last

            def h1T_high(b, at):
                act.wait_ge(h1tr_done, nth(b, 1, 1))
                act.wait_ge(pa_ready, nth(b, 1, 1))
                tiles(h1T[0], at, ACT.Copy, lambda f: par_a[:, T_G1 + f:T_G1 + f + 1], scale=True).then_inc(h1T_hi, 1)

            def h1T_whole(b, at):
                tiles(h1T_f, at, ACT.Copy, lambda f: par_a[:, T_G1 + f:T_G1 + f + 1], scale=True)\
                    .then_inc(h1T_f_ready, 1)

            def h2T_high(b, par_):
                act.wait_ge(h2tr_done, nth(b, 1, 1))
                outs = ((h2T[0], h2T_hi), (h2T_f, h2T_f_ready))
                for out_, done in outs[:1] if final(b) else outs:
                    tiles(out_, Y, ACT.Copy, lambda f: g2_column(par_, f), scale=True).then_inc(done, 1)

            def q_high(b):
                act.wait_ge(q_done, nth(b, 1, 1))
                if later(b):
                    act.wait_ge(q_saved, nth(b, 48, 0))
                tiles(qk_parts[:, 0, 0], B_Q, ACT.Identity, lambda f: par_a[:, T_QB + f:T_QB + f + 1]).then_inc(q_hi, 1)

            def k_high(b):
                act.wait_ge(k_done, nth(b, 1, 1))
                if later(b):
                    act.wait_ge(k_saved, nth(b, 48, 0))
                tiles(qk_parts[:, 1, 0], B_K, ACT.Identity, lambda f: par_a[:, T_KB + f:T_KB + f + 1]).then_inc(k_hi, 1)

            def copy_v(b, par_):
                act.wait_ge(v_done, nth(b, 1, 1))
                for t in range(TT):
                    last = act.activation(v_aug[par_][:, t, :, 0:DH],
                                          PS[:, B_V, t * D:(t + 1) * D].rearrange("p (h n) -> p h n", n=DH), ACT.Copy)
                last.then_inc(v_ready, 1)

            def copy_negmax(i):
                act.wait_ge(mtr_done, nth(i, 1, 1))
                if later(i):
                    act.wait_ge(m_stacked, nth(i, 16, 0))
                act.activation(negmaxT[:, :], PS[0:NH, X, 0:P], ACT.Copy).then_inc(negmaxT_ready, 1)

            def copy_o(i, pair_):
                act.wait_ge(pv_done, nth(i, SET, 2 * pair_ + 2))
                act.activation(o_aug[:, 2 * pair_:2 * pair_ + 2, :].rearrange("p s n -> p (s n)"), bank(VAL), ACT.Copy)\
                   .then_inc(o_copied, 1)

            def table(func):
                act.activation(scrap[:, 1:2], scrap[:, 0:1], func)

            def gelu(c, par_, m):
                act.wait_ge(f1_done, nth(c, 4, m + 1))
                for f in range(2):
                    col = T_F1 - NPAR_A + 2 * m + f
                    last = act.activation(gelu_f[:, 2 * m + f, :], PS[:, F1_BANKS[m], f * P:(f + 1) * P],
                                          ACT.Gelu_apprx_tanh, bias=par_t[par_][:, col:col + 1])
                last.then_inc(gelu_done, 1)
                two = slice(2 * m, 2 * m + 2)
                act.wait_ge(gelu_done, nth(c, 4, m + 1))
                act.activation(g_hi[:, two, :], gelu_f[:, two, :], ACT.Copy).then_inc(g_hi_done, 1)

            def phase1(i, par_):
                b, a, c = i + 1, i - 1, i - 2
                if real(b):
                    q_high(b)
                if real(a):
                    copy_o(a, 1)
                if real(i):
                    copy_negmax(i)
                if real(c):
                    table(ACT.Gelu_apprx_tanh)
                if real(b):
                    k_high(b)
                    copy_v(b, 1 - par_)
                if real(i + 2):
                    relu(i + 2, B_F)
                if real(c) and not real(b):
                    gelu(c, par_, 0)
                if real(a):
                    act.wait_ge(ontr_done, nth(a, 1, 1))
                    act.wait_ge(pt_ready, nth(a, 1, 1))
                    tiles(oT[0], M0, ACT.Identity, lambda f: vb_column(1 - par_, f)).then_inc(oT_hi, 1)
                if real(c):
                    if real(b):
                        act.wait_ge(q_saved, nth(b, 48, 48))
                        gelu(c, par_, 0)
                    gelu(c, par_, 1)
                    if real(b):
                        act.wait_ge(k_saved, nth(b, 48, 48))
                    gelu(c, par_, 2)
                    gelu(c, par_, 3)
                    if real(i):
                        table(ACT.Exp)
                if real(a) and not bare(i):
                    h2T_high(a, 1 - par_)

            def phase2(i, par_):
                a, c = i - 1, i - 2
                if not real(i):
                    return
                if real(c):
                    act.wait_ge(g_lo_done, nth(c, 4, 4))
                for n in range(ST_STEPS):
                    s, j = n // SET_STEPS, n % SET_STEPS
                    act.wait_ge(st_done, nth(i, ST_STEPS, n + 1))
                    if s >= 2 and j == 0:
                        act.wait_ge(pv_done, nth(i, SET, s - 1))
                    act.activation(probs[s % 2][:, j].rearrange("p t q -> p (t q)"), bank(n % S_BANKS), ACT.Exp,
                                   scale=DH ** -0.5).then_inc(exp_done, 1)
                    if n == 11:
                        copy_o(i, 0)
                    if n == 2 and real(i + 2):
                        h1T_high(i + 2, X)
                    if n == H2T_AT and bare(i):
                        h2T_high(a, 1 - par_)
                    if n == 5 and real(i + 2):
                        h1T_whole(i + 2, X)

            def copy_delta(n):
                act.wait_ge(delta_done, 2 * n + 2)
                if n >= 2:
                    act.wait_ge(deltaT_done, n - 1)
                act.activation(dtmp[:, n % 2, :], bank(n % 2), ACT.Copy).then_inc(delta_copied, 1)

            def weights_high(n, w):
                act.wait_ge(ld_ring[n % RING], 16 * (n // RING + 1))
                size = w[0].shape[1] * w[0].shape[2]
                act.activation(w[0][:, :, :].rearrange("p k n -> p (k n)"), ring[:, n % RING, 0:size], ACT.Copy)\
                   .then_inc(w_hi, 1)

            act.wait_ge(ld_const, 16 * 4)
            act.wait_ge(pe_cond, 1)
            for f in range(KT):
                last = act.activation(s1[:, f, :], PS[:, M1, f * B:(f + 1) * B], ACT.Silu,
                                      bias=cols[:, C_BT1 + f:C_BT1 + f + 1])
            last.then_inc(act_cond, 1)
            act.wait_ge(dve_cond, 1)
            act.activation(s2[:, :, :], z2[:, :, :], ACT.Silu).then_inc(act_cond, 1)
            copy_delta(0)
            copy_delta(1)
            act.wait_ge(ld_wqkv, 16)
            act.activation(wqkv[0][:, :, :], wqkv_f, ACT.Copy).then_inc(w_hi, 1)
            for n in range(2, NCHUNK // 2):
                copy_delta(n)
                if n == 5:
                    relu(0, X)
            relu(1, Y)
            h1T_high(0, X)
            q_high(0)
            k_high(0)
            copy_v(0, 0)
            h1T_high(1, Y)
            weights_high(NCHUNK, wf1)
            q_high(1)
            k_high(1)
            relu(2, B_F)
            weights_high(NCHUNK + 1, wf2)
            weights_high(NCHUNK + 2, wo)
            act.wait_ge(pool_init, 5)
            table(ACT.Exp)
            copy_v(1, 1)
            copy_negmax(0)
            act.wait_ge(w_lo, 4)
            phase2(0, 0)
            phase1(1, 1)
            phase2(1, 1)
            with act.Fori(2, B - 3, 2) as j:
                for u in range(2):
                    phase1(j + u, u)
                    phase2(j + u, u)
            for i in range(B - 2, B + 2):
                phase1(i, i % 2)
                phase2(i, i % 2)

        @block.vector
        def _(dve):
            def cut(lo, x, hi):
                return dve.tensor_tensor(lo, x, hi.bitcast(FP32), ALU.subtract)

            def stats(b, x, ready, bn, bn_ready, mv, st_ready):
                dve.wait_ge(ready, nth(b, 1, 1))
                for t in range(TT):
                    last = dve.bn_stats(bn[:, t, :], x[:, t, :])
                last.then_inc(bn_ready, 1)
                dve.wait_ge(init_done, 1)
                dve.wait_ge(bn_ready, nth(b, 1, 1))
                for t in range(TT):
                    last = dve.bn_aggr(mv[:, t, :], bn[:, t, :])
                last.then_inc(st_ready, 1)

            def normalise(b, h, x, mv, rs, rs_ready, h_ready):
                dve.wait_ge(rs_ready, nth(b, 1, 1))
                for t in range(TT):
                    last = dve.tensor_scalar(h[:, t, :], x[:, t, :], mv[:, t, 0:1], rs[:, t:t + 1],
                                             ALU.subtract, ALU.mult)
                last.then_inc(h_ready, 1)

            def low_part(b, hi_ready, lo_ready, lo, hi, at, column, op):
                dve.wait_ge(hi_ready, nth(b, 1, 1))
                for f in range(KT):
                    last = dve.scalar_tensor_tensor(lo[:, f, :], PS[:, at, f * P:(f + 1) * P], column(f),
                                                    hi[:, f, :].bitcast(FP32), op, ALU.subtract)
                last.then_inc(lo_ready, 1)

            def adapter_down(b):
                if later(b):
                    dve.wait_ge(down_done, nth(b, 1, 0))
                dve.tensor_copy(wd_cur, w_ad[:, bass.ds(b, 1), 0:D].rearrange("p o (k n) -> p (o k) n", k=KT))\
                   .then_inc(wd_ready, 1)

            def parameters_a(b):
                if later(b):
                    dve.wait_ge(k_hi, nth(b, 1, 0))
                    dve.wait_ge(k_lo, nth(b, 1, 0))
                dve.tensor_copy(par_a[:, :], par[:, bass.ds(b, 1), 0:NPAR_A].rearrange("p o n -> p (o n)"))\
                   .then_inc(pa_ready, 1)

            def x1_sum(b, par_, at):
                dve.wait_ge(up_done, nth(b, 1, 1))
                dve.wait_ge(xb_ready, nth(b, 1, 1))
                dve.tensor_tensor(x_in[par_], bank(at).rearrange("p (t n) -> p t n", t=TT), x_in[par_], ALU.add)\
                   .then_inc(x1_ready, 1)

            def stats1(b, par_):
                stats(b, x_in[par_], x1_ready, bn1, bns1_ready, mv1, st1_ready)

            def norm1(b, par_):
                if later(b):
                    dve.wait_ge(h1tr_done, nth(b, 1, 0))
                normalise(b, h1, x_in[par_], mv1, rs1, rs1_ready, h1_ready)

            def h1T_low(b, at):
                low_part(b, h1T_hi, h1T_lo, h1T[1], h1T[0], at, lambda f: par_a[:, T_G1 + f:T_G1 + f + 1], ALU.mult)

            def h2T_low(b, par_):
                low_part(b, h2T_hi, h2T_lo, h2T[1], h2T[0], Y, lambda f: g2_column(par_, f), ALU.mult)

            def q_low(b):
                low_part(b, q_hi, q_lo, qk_parts[:, 0, 1], qk_parts[:, 0, 0], B_Q,
                         lambda f: par_a[:, T_QB + f:T_QB + f + 1], ALU.add)

            def k_low(b):
                low_part(b, k_hi, k_lo, qk_parts[:, 1, 1], qk_parts[:, 1, 0], B_K,
                         lambda f: par_a[:, T_KB + f:T_KB + f + 1], ALU.add)

            def o_divided(a, par_):
                dve.wait_ge(otr_done, nth(a, 1, 1))
                o4 = PS[:, M0:M0 + 2, :].rearrange("p t (h n) -> p t h n", n=32)
                dve.reciprocal(rden[:, :, :], o4[:, :, :, DH]).then_inc(rden_ready, 1)
                dve.wait_ge(rden_ready, nth(a, 1, 1))
                for t in range(TT):
                    last = dve.tensor_tensor(o_tok[:, t, :].rearrange("p (h n) -> p h n", n=DH), o4[:, t, :, 0:DH],
                                             rden[:, t, :].unsqueeze(2).to_broadcast([128, NH, DH]), ALU.mult)
                last.then_inc(o_ready, 1)

            def residual(a, par_):
                dve.wait_ge(wo_done, nth(a, 1, 1))
                dve.wait_ge(x2base_ready, nth(a, 1, 1))
                dve.tensor_tensor(h2, bank(M1).rearrange("p (t n) -> p t n", t=TT), each_tile(a12[par_][:, 0, :]),
                                  ALU.mult)\
                   .then_inc(a1o_ready, 1)
                dve.wait_ge(a1o_ready, nth(a, 1, 1))
                dve.tensor_tensor(x2[par_], x2[par_], h2, ALU.add).then_inc(x2_ready, 1)

            def gelu_cut(c, m):
                two = slice(2 * m, 2 * m + 2)
                dve.wait_ge(g_hi_done, nth(c, 4, m + 1))
                cut(g_lo[:, two, :], gelu_f[:, two, :], g_hi[:, two, :]).then_inc(g_lo_done, 1)

            def mlp_end(c, par_):
                dve.wait_ge(f2_done, nth(c, 1, 1))
                if later(c):
                    dve.wait_ge(x3_ready, nth(c, 1, 0))
                dve.tensor_tensor(a2y, bank(VAL).rearrange("p (t n) -> p t n", t=TT), each_tile(a12[par_][:, 1, :]),
                                  ALU.mult)\
                   .then_inc(a2y_ready, 1)
                if final(c):
                    dve.wait_ge(x2b_ready, nth(c, 1, 1))
                    dve.wait_ge(a2y_ready, nth(c, 1, 1))
                    dve.tensor_tensor(x2[par_], x2[par_], a2y, ALU.add).then_inc(x3_ready, 1)

            def phase1(i, par_):
                b, a, c = i + 1, i - 1, i - 2
                if real(i + 2):
                    adapter_down(i + 2)
                if real(b):
                    q_low(b)
                if real(a):
                    if later(a, 2):
                        dve.wait_ge(gelu_done, nth(a - 1, 4, 0))
                    dve.tensor_copy(par_t[1 - par_][:, :],
                                    par[:, bass.ds(a, 1), NPAR_A:NPAR].rearrange("p o n -> p (o n)"))\
                       .then_inc(pt_ready, 1)
                    o_divided(a, 1 - par_)
                if real(b):
                    k_low(b)
                if real(a):
                    low_part(a, oT_hi, oT_lo, oT[1], oT[0], M0, lambda f: vb_column(1 - par_, f), ALU.add)
                if real(i + 2):
                    x1_sum(i + 2, par_, B_F)
                if real(c):
                    gelu_cut(c, 0)
                if real(i + 2):
                    stats1(i + 2, par_)
                if real(a):
                    residual(a, 1 - par_)
                if real(c):
                    gelu_cut(c, 1)
                if real(i + 2):
                    norm1(i + 2, par_)
                if real(a):
                    stats(a, x2[1 - par_], x2_ready, bn2, bns2_ready, mv2, st2_ready)
                if real(c):
                    gelu_cut(c, 2)
                if bare(i):
                    for n in range(AHEAD):
                        row_max(b, n)
                if real(a):
                    normalise(a, h2, x2[1 - par_], mv2, rs2, rs2_ready, h2_ready)
                if real(c):
                    gelu_cut(c, 3)
                if final(a):
                    h2T_low(a, 1 - par_)
                if real(i + 2):
                    parameters_a(i + 2)
                if real(b) and not bare(i):
                    for n in range(AHEAD):
                        row_max(b, n)

            def row_max(b, n, banks=MAX_BANKS):
                s, t, j = n // 4, n // 2 % 2, 2 * (n % 2)
                g, half = s // HALF, s % HALF
                at = half * PP * G + j * G + g
                dve.wait_ge(sm_done, nth(b, SM_STEPS, n + 1))
                dve.tensor_reduce(negmax[:, t, at:at + G + 1:G],
                                  bank(banks[n % len(banks)]).rearrange("p (j n) -> p j n", j=2),
                                  AX.X, ALU.max, negate=True).then_inc(sm_read, 1)

            def phase2(i, par_):
                a, c = i - 1, i - 2
                if real(c):
                    mlp_end(c, par_)
                for n in range(AHEAD, SM_STEPS):
                    if real(i + 1):
                        row_max(i + 1, n)

            for i in range(2):
                dve.memset(k_stack[i][MROW:MROW + 1].bitcast(FP32), 1.0).then_inc(ones_set, 1)
            dve.wait_ge(ld_const, 16 * 4)
            dve.wait_ge(pe_cond, 2)
            for f in range(KT):
                last = dve.scalar_tensor_tensor(z2[:, f, :], PS[:, VAL, f * B:(f + 1) * B], cols[:, C_BT2 + f:C_BT2 + f + 1],
                                                cols[:, C_EMB + f * B:C_EMB + (f + 1) * B], ALU.add, ALU.add)
            last.then_inc(dve_cond, 1)

            def add_delta(n):
                w = n // 4
                if n == 0:
                    dve.scalar_tensor_tensor(base[:, 0:512], base[:, 512:1024], DELTA_SCALE, base[:, 0:512],
                                             ALU.mult, ALU.add).then_inc(init_done, 1)
                    dve.wait_ge(init_done, 1)
                dve.wait_ge(deltaT_done, n + 1)
                c0 = n * 64
                dve.scalar_tensor_tensor(w_ad[:, :, c0:c0 + 64].rearrange("p b c -> p c b"),
                                         bank(2 + n % 2).rearrange("p (c b) -> p c b", b=B), DELTA_SCALE,
                                         base[:, c0:c0 + 64].unsqueeze(2).to_broadcast([128, 64, B]),
                                         ALU.mult, ALU.add).then_inc(delta_ready, 1)

            add_delta(0)
            dve.wait_ge(pe_cond, 3)
            dve.tensor_tensor(mod[:, :, :], PS[:, M1, 0:8 * B].rearrange("p (c b) -> p c b", b=B),
                              cols[:, C_BC:C_BC + 8 * B].rearrange("p (c b) -> p c b", b=B), ALU.add).then_inc(dve_cond, 1)
            dve.wait_ge(pe_cond, 4)
            dve.wait_ge(ld_wc, 32)
            dve.tensor_tensor(a_sb[:, :], PS[0:B, VAL, :], a_sb[:, :], ALU.add).then_inc(dve_cond, 1)
            add_delta(1)
            dve.wait_ge(w_hi, 1)
            cut(wqkv[1][:, :, :], wqkv_f, wqkv[0][:, :, :]).then_inc(w_lo, 1)
            dve.wait_ge(dve_cond, 2)
            dve.tensor_copy(par[:, :, T_G1:T_G1 + 2].rearrange("p b c -> p c b"), mod[:, 0:2, :])
            dve.tensor_copy(par[:, :, T_G2:T_G2 + 2].rearrange("p b c -> p c b"), mod[:, 4:6, :])
            dve.wait_ge(pe_cond, 5)
            dve.tensor_tensor(par[:, :, T_QB:T_QB + 6].rearrange("p b c -> p c b"),
                              PS[:, M1, 0:6 * B].rearrange("p (c b) -> p c b", b=B),
                              cols[:, C_BQKV:C_BQKV + 6 * B].rearrange("p (c b) -> p c b", b=B), ALU.add).then_inc(dve_cond, 1)
            dve.wait_ge(dve_cond, 4)
            parameters_a(0)
            add_delta(2)
            for i in range(2):
                last = dve.memset(v_aug[i][:, :, :, DH:32], 1.0)
            last.then_inc(init_done, 1)
            add_delta(3)
            dve.wait_ge(delta_ready, 4)
            adapter_down(0)
            for n in range(4, NCHUNK // 2):
                add_delta(n)
                if n == 6:
                    adapter_down(1)
            x1_sum(0, 0, X)
            stats1(0, 0)
            norm1(0, 0)
            x1_sum(1, 1, Y)
            stats1(1, 1)
            h1T_low(0, X)
            norm1(1, 1)
            q_low(0)
            k_low(0)
            parameters_a(1)
            h1T_low(1, Y)
            q_low(1)
            k_low(1)
            dve.wait_ge(pe_cond, 6)
            dve.tensor_tensor(par[:, :, T_F1:T_F1 + FT].rearrange("p b c -> p c b"),
                              PS[:, VAL, 0:FT * B].rearrange("p (c b) -> p c b", b=B),
                              cols[:, C_BF1:C_BF1 + FT * B].rearrange("p (c b) -> p c b", b=B), ALU.add).then_inc(dve_cond, 1)
            adapter_down(2)
            for n in range(SM_STEPS):
                row_max(0, n, MAX_BANKS_0)
            x1_sum(2, 0, B_F)
            stats1(2, 0)
            parameters_a(2)
            dve.wait_ge(dve_cond, 5)
            for n in range(AHEAD):
                row_max(1, n)
            norm1(2, 0)
            phase2(0, 0)
            phase1(1, 1)
            phase2(1, 1)
            with dve.Fori(2, B - 3, 2) as j:
                for u in range(2):
                    phase1(j + u, u)
                    phase2(j + u, u)
            for i in range(B - 2, B + 2):
                phase1(i, i % 2)
                phase2(i, i % 2)

        @block.tensor
        def _(pe):
            def three(out, terms, first=True, last=True, **kw):
                n = len(terms)
                for i, (lhs, rhs) in enumerate(terms):
                    for a, c in ((0, 0), (0, 1), (1, 0)):
                        m = pe.matmul(out, lhs[a], rhs[c], start=first and i == 0 and a == c == 0,
                                      stop=last and i == n - 1 and a == 1, **kw)
                return m

            def pair(x, *at):
                return [p[at] for p in x]

            full = slice(None)

            def down(b, at):
                pe.wait_ge(ld_xT, nth(b, 16, 16))
                pe.wait_ge(wd_ready, nth(b, 1, 1))
                for k in range(KT):
                    m = pe.matmul(PS[:, at, 0:P], wd_cur[:, k, :], xT[:, k, :], start=k == 0, stop=k == KT - 1)
                m.then_inc(down_done, 1)

            def up(b, at):
                pe.wait_ge(relu_ready, nth(b, 1, 1))
                for t in range(TT):
                    m = pe.matmul(PS[:, at, t * D:(t + 1) * D], downT[:, t * 128:(t + 1) * 128],
                                  w_ad[:, bass.ds(b, 1), D:2 * D].rearrange("p o n -> p (o n)"), start=True, stop=True)
                m.then_inc(up_done, 1)

            def transpose4(out, x):
                for f in range(KT):
                    for t in range(TT):
                        m = pe.transpose(out[:, f * P + t * 128:f * P + (t + 1) * 128], x[:, t, f * 128:(f + 1) * 128],
                                         ident[:, :])
                return m

            def h1_transpose(b, at):
                pe.wait_ge(h1_ready, nth(b, 1, 1))
                transpose4(bank(at), h1).then_inc(h1tr_done, 1)

            def h2_transpose(a):
                pe.wait_ge(h2_ready, nth(a, 1, 1))
                transpose4(bank(Y), h2).then_inc(h2tr_done, 1)

            def project_tile(w, at, g):
                c = slice((w * G + g) * 128, (w * G + g + 1) * 128)
                return three(PS[:, at, g * P:(g + 1) * P],
                             [(pair(wqkv, full, k, c), pair(h1T, full, k, full)) for k in range(KT)])

            def project_q():
                project_tile(0, B_Q, 0)
                project_tile(0, B_Q, 1).then_inc(q_done, 1)

            def project_k(between=None):
                project_tile(1, B_K, 0)
                if between is not None:
                    o_transpose(between)
                project_tile(1, B_K, 1).then_inc(k_done, 1)

            def project_v():
                for t in range(TT):
                    c = slice(t * 128, (t + 1) * 128)
                    m = three(PS[:, B_V, t * D:(t + 1) * D],
                              [(pair(h1T, full, k, c), pair(wqkv, full, k, slice(2 * D, 3 * D))) for k in range(KT)])
                m.then_inc(v_done, 1)

            def negmax_transpose(i):
                pe.wait_ge(sm_read, nth(i, SM_STEPS, SM_STEPS))
                for t in range(TT):
                    m = pe.transpose(PS[0:NH, X, t * 128:(t + 1) * 128], negmax[:, t, :], ident[:, :])
                m.then_inc(mtr_done, 1)

            def o_transpose(a):
                pe.wait_ge(o_copied, nth(a, 2, 2))
                for t in range(TT):
                    for s in range(SET):
                        m = pe.transpose(PS[:, M0 + t, s * 128:(s + 1) * 128], o_aug[:, s, t * 128:(t + 1) * 128],
                                         ident[:, :])
                m.then_inc(otr_done, 1)

            def o_back(a):
                pe.wait_ge(o_ready, nth(a, 1, 1))
                transpose4(bank(M0), o_tok).then_inc(ontr_done, 1)

            def project_o(a):
                pe.wait_ge(oT_hi, nth(a, 1, 1))
                pe.wait_ge(oT_lo, nth(a, 1, 1))
                for t in range(TT):
                    c = slice(t * 128, (t + 1) * 128)
                    m = three(PS[:, M1, t * D:(t + 1) * D],
                              [(pair(oT, full, k, c), pair(wo, full, k, full)) for k in range(KT)])
                m.then_inc(wo_done, 1)

            def mlp_in(c, m4):
                if m4 == 0:
                    pe.wait_ge(h2T_hi, nth(c, 1, 1))
                    pe.wait_ge(h2T_lo, nth(c, 1, 1))
                elif m4 >= 2:
                    pe.wait_ge(gelu_done, nth(c, 4, m4 - 1))
                for f in range(2):
                    col = slice((2 * m4 + f) * 128, (2 * m4 + f + 1) * 128)
                    m = three(PS[:, F1_BANKS[m4], f * P:(f + 1) * P],
                              [(pair(wf1, full, k, col), pair(h2T, full, k, full)) for k in range(KT)])
                m.then_inc(f1_done, 1)

            def mlp_out(c, a, b, par_):
                for k in range(FT):
                    if k == 6 and real(a):
                        h2_transpose(a)
                    if k == 7 and real(b):
                        for n in range(AHEAD):
                            max_step(b, 1 - par_, n)
                    if k % 2 == 0:
                        pe.wait_ge(g_lo_done, nth(c, 4, k // 2 + 1))
                    for t in range(TT):
                        col = slice(t * 128, (t + 1) * 128)
                        m = three(PS[:, VAL, t * D:(t + 1) * D],
                                  [(pair((g_hi, g_lo), full, k, col), pair(wf2, full, k, full))],
                                  first=k == 0 and t == 0, last=k == FT - 1, skip_group_check=True)
                m.then_inc(f2_done, 1)

            def max_step(b, par_, n, banks=MAX_BANKS):
                s, t, j = n // 4, n // 2 % 2, 2 * (n % 2)
                g, half = s // HALF, s % HALF
                if n == 0:
                    pe.wait_ge(q_stacked, nth(b, STACK_DMAS * 16, STACK_DMAS * 16))
                    pe.wait_ge(k_stacked, nth(b, STACK_DMAS * 16, STACK_DMAS * 16))
                if n == 1 and later(b, 2):
                    pe.wait_ge(a1o_ready, nth(b - 2, 1, 1))
                if n >= len(banks):
                    pe.wait_ge(sm_read, nth(b, SM_STEPS, n - len(banks) + 1))
                for p in range(2):
                    m = pe.matmul(PS[:, banks[n % len(banks)], p * P:(p + 1) * P],
                                  q_stack[par_][0:MROW, half, j + p, g, t * 128:(t + 1) * 128],
                                  k_stack[par_][0:MROW, j + p, g, :], start=True, stop=True)
                m.then_inc(sm_done, 1)

            def score_step(b, par_, n):
                s, j = n // SET_STEPS, n % SET_STEPS
                g, half = s // HALF, s % HALF
                if n >= S_BANKS:
                    pe.wait_ge(exp_done, nth(b, ST_STEPS, n - S_BANKS + 1))
                for t in range(TT):
                    m = pe.matmul(PS[:, n % S_BANKS, t * P:(t + 1) * P],
                                  k_stack[par_][0:MROW + 1, j, g, t * 128:(t + 1) * 128],
                                  q_stack[par_][0:MROW + 1, half, j, g, :], start=True, stop=True)
                m.then_inc(st_done, 1)

            def values(b, par_, s, t):
                if t == 0:
                    pe.wait_ge(exp_done, nth(b, ST_STEPS, SET_STEPS * (s + 1)))
                    if s == 2:
                        pe.wait_ge(o_copied, nth(b, 2, 1))
                for j in range(PP):
                    m = pe.matmul(PS[32 * j:32 * j + 32, VAL, s % 2 * P:(s % 2 + 1) * P],
                                  v_aug[par_][:, t, s * PP + j, :], probs[s % 2][:, j, t, :],
                                  start=t == 0, stop=t == TT - 1)
                if t == TT - 1:
                    m.then_inc(pv_done, 1)

            def phase1(i, par_):
                b, a, c = i + 1, i - 1, i - 2
                if real(b):
                    pe.wait_ge(h1T_hi, nth(b, 1, 1))
                    pe.wait_ge(h1T_lo, nth(b, 1, 1))
                    pe.wait_ge(exp_done, nth(a, ST_STEPS, ST_STEPS - 2))
                    project_q()
                if real(a):
                    values(a, 1 - par_, SET - 1, 0)
                    values(a, 1 - par_, SET - 1, 1)
                if real(i):
                    negmax_transpose(i)
                if real(b):
                    project_k(between=a)
                    project_v()
                elif real(c):
                    mlp_in(c, 0)
                if real(a) and not real(b):
                    o_transpose(a)
                if real(i + 2):
                    pe.wait_ge(q_lo, nth(b, 1, 1))
                    down(i + 2, B_F)
                if real(a) and real(b):
                    o_back(a)
                if real(c) and real(b):
                    mlp_in(c, 0)
                if real(i + 2):
                    up(i + 2, B_F)
                if real(c):
                    if real(i):
                        pe.wait_ge(negmaxT_ready, nth(i, 1, 1))
                    mlp_in(c, 1)
                if real(a) and not real(b):
                    o_back(a)
                    mlp_in(c, 2)
                if real(a):
                    project_o(a)
                if real(c):
                    if real(b) or not real(a):
                        mlp_in(c, 2)
                    mlp_in(c, 3)
                    mlp_out(c, a, b, par_)
                else:
                    if real(a) and not bare(i):
                        h2_transpose(a)
                    if real(b):
                        for n in range(AHEAD):
                            max_step(b, 1 - par_, n)

            def phase2(i, par_):
                a, c = i - 1, i - 2
                if not real(i):
                    if real(a):
                        pe.wait_ge(a2y_ready, nth(c, 1, 1))
                    return
                if real(i + 1):
                    pe.wait_ge(q_lo, nth(i + 1, 1, 1))
                    pe.wait_ge(k_lo, nth(i + 1, 1, 1))
                    pe.wait_ge(v_ready, nth(i + 1, 1, 1))
                if real(i + 2):
                    pe.wait_ge(x1_ready, nth(i + 2, 1, 1))
                pe.wait_ge(m_stacked, nth(i, 16, 16))
                for n in range(ST_STEPS):
                    score_step(i, par_, n)
                    if real(i + 1) and n + AHEAD < SM_STEPS:
                        max_step(i + 1, 1 - par_, n + AHEAD)
                    if n == 1 and real(i + 2):
                        h1_transpose(i + 2, X)
                    if n == H2_AT and bare(i):
                        h2_transpose(a)
                    s, t = (n - 5) // SET_STEPS, (n - 5) % SET_STEPS / 2
                    if n >= 5 and t in (0, 1):
                        if n == 5 and real(c):
                            pe.wait_ge(a2y_ready, nth(c, 1, 1))
                        values(i, par_, s, int(t))

            def delta_chunk(n):
                b2, half = n // 2, n % 2
                pe.wait_ge(ld_ring[n % RING], 16 * (n // RING + 1))
                if half == 0 and b2 >= 2:
                    pe.wait_ge(delta_copied, b2 - 1)
                data = ring[:, n % RING, :].rearrange("p (k j n) -> p k j n", k=KH, j=2)
                for k in range(KH):
                    for j in range(2):
                        at = 32 * (2 * half + j)
                        m = pe.matmul(PS[at:at + 32, b2 % 2, :], hbd[:, k, :], data[:, k, j, :],
                                      start=k == 0, stop=k == KH - 1)
                m.then_inc(delta_done, 1)

            def delta_transpose(n):
                pe.wait_ge(delta_copied, n + 1)
                if n >= 2:
                    pe.wait_ge(delta_ready, n - 1)
                for c in range(4):
                    m = pe.transpose(PS[:, 2 + n % 2, c * 128:(c + 1) * 128], dtmp[:, n % 2, c * 128:(c + 1) * 128],
                                     ident[:, :])
                m.then_inc(deltaT_done, 1)

            def columns(at, tiles, w, x):
                for c in range(tiles):
                    for k in range(KT):
                        m = pe.matmul(PS[:, at, c * B:(c + 1) * B], w[:, k, c * 128:(c + 1) * 128],
                                      x[:, k, :], start=k == 0, stop=k == KT - 1)
                return m

            pe.wait_ge(ld_const, 16 * 4)
            pe.wait_ge(ld_small, 16)
            for f in range(KT):
                m = pe.matmul(PS[:, M1, f * B:(f + 1) * B], wt1[:, f * 128:(f + 1) * 128], cond_t, start=True, stop=True)
            m.then_inc(pe_cond, 1)
            delta_chunk(0)
            pe.wait_ge(act_cond, 1)
            columns(VAL, KT, wt2, s1).then_inc(pe_cond, 1)
            delta_chunk(1)
            delta_transpose(0)
            delta_chunk(2)
            pe.wait_ge(act_cond, 2)
            pe.wait_ge(ld_wc, 32)
            columns(M1, 8, wc, s2).then_inc(pe_cond, 1)
            for k in range(KT):
                m = pe.matmul(PS[0:B, VAL, :], s2[:, k, :], wc[:, k, 4 * D:6 * D], start=k == 0, stop=k == KT - 1)
            m.then_inc(pe_cond, 1)
            delta_chunk(3)
            delta_transpose(1)
            delta_chunk(4)
            pe.wait_ge(ld_wqkv, 16)
            pe.wait_ge(dve_cond, 2)
            columns(M1, 6, wqkv_f, mod[:, 2:4, :]).then_inc(pe_cond, 1)
            delta_chunk(5)
            for n in range(3, NCHUNK // 2):
                delta_transpose(n - 1)
                delta_chunk(2 * n)
                delta_chunk(2 * n + 1)
                if n == 5:
                    down(0, X)
            delta_transpose(NCHUNK // 2 - 1)
            down(1, Y)
            pe.wait_ge(delta_ready, NCHUNK // 2)
            up(0, X)
            up(1, Y)
            h1_transpose(0, X)
            pe.wait_ge(h1T_hi, 1)
            pe.wait_ge(h1T_lo, 1)
            pe.wait_ge(w_lo, 1)
            project_q()
            project_k()
            project_v()
            h1_transpose(1, Y)
            pe.wait_ge(ld_ring[NCHUNK % RING], 16 * (NCHUNK // RING + 1))
            pe.wait_ge(dve_cond, 3)
            columns(VAL, 8, wf1_f, mod[:, 6:8, :]).then_inc(pe_cond, 1)
            pe.wait_ge(h1T_hi, 2)
            pe.wait_ge(h1T_lo, 2)
            pe.wait_ge(q_lo, 1)
            pe.wait_ge(k_lo, 1)
            pe.wait_ge(v_ready, 1)
            project_q()
            project_k()
            for n in range(SM_STEPS):
                max_step(0, 0, n, MAX_BANKS_0)
                if n == 3:
                    pe.wait_ge(q_lo, 2)
                    down(2, B_F)
                if n == 7:
                    up(2, B_F)
            project_v()
            negmax_transpose(0)
            pe.wait_ge(ones_set, 2)
            pe.wait_ge(dve_cond, 5)
            for n in range(AHEAD):
                max_step(1, 1, n)
            phase2(0, 0)
            pe.wait_ge(w_lo, 4)
            phase1(1, 1)
            phase2(1, 1)
            with pe.Fori(2, B - 3, 2) as j:
                for u in range(2):
                    phase1(j + u, u)
                    phase2(j + u, u)
            for i in range(B - 2, B + 2):
                phase1(i, i % 2)
                phase2(i, i % 2)


def kernel(x, cond_256, fside_BxS_0, L0_cond_Wd, L0_cond_bd, L0_cond_Wu, L0_cond_bu, L0_cond_Wdd, L0_cond_bdd,
           L0_cond_Wdu, L0_cond_bdu, L1_cond_W_t1, L1_cond_b_t1, L1_cond_W_t2, L1_cond_b_t2, L1_cond_W_c,
           L1_cond_b_c, L1_cond_W_qkv, L1_cond_b_qkv, L1_cond_W_o, L1_cond_b_o, L1_cond_W_f1, L1_cond_b_f1,
           L1_cond_W_f2, L1_cond_b_f2):
    import numpy as np
    import concourse.bacc as bacc
    from concourse.bass_utils import run_bass_kernel_spmd as run

    (x, h, c, Wd, bd, Wu, bu, Wdd, bdd, Wdu, bdu, Wt1, bt1, Wt2, bt2, Wc, bc, Wqkv, bqkv, Wo, bo, Wf1, bf1, Wf2,
     bf2) = (np.asarray(a) for a in (
         x, cond_256, fside_BxS_0, L0_cond_Wd, L0_cond_bd, L0_cond_Wu, L0_cond_bu, L0_cond_Wdd, L0_cond_bdd,
         L0_cond_Wdu, L0_cond_bdu, L1_cond_W_t1, L1_cond_b_t1, L1_cond_W_t2, L1_cond_b_t2, L1_cond_W_c,
         L1_cond_b_c, L1_cond_W_qkv, L1_cond_b_qkv, L1_cond_W_o, L1_cond_b_o, L1_cond_W_f1, L1_cond_b_f1,
         L1_cond_W_f2, L1_cond_b_f2))

    def by_tile(w):
        return w.reshape(-1, 128, w.shape[1]).transpose(1, 0, 2)

    def column(v, repeat=1):
        return np.repeat(v.reshape(-1, 128).T, repeat, axis=1)

    cols = np.concatenate([column(bd), column(bt1), column(bt2), by_tile(c.T).reshape(128, -1),
                           column(bc[:4 * D], B), column(bqkv, B), column(bf1, B)], axis=1)
    hbd = np.zeros((4, 32, KH, 4, B), h.dtype)
    for j in range(4):
        hbd[j, :, :, j, :] = h.T.reshape(KH, 32, B).transpose(1, 0, 2)
    small = np.zeros((128, 768 + B), h.dtype)
    small[:HC, 0:256] = Wt1.T
    small[:, 256:768] = by_tile(Wt2.T).reshape(128, -1)
    small[:HC, 768:] = h.T
    def down_columns(w):
        return w.reshape(BN, KT, 128, -1).transpose(2, 1, 0, 3).reshape(128, 2 * 128, -1)

    def up_columns(w):
        return w.reshape(D, BN, -1).transpose(1, 0, 2)
    base = np.concatenate([f(w)[:, :, 0] for w_ in ((Wd, Wu), (bdd, bdu)) for f, w in zip((down_columns, up_columns), w_)],
                          axis=1)
    gen = np.concatenate([down_columns(Wdd), up_columns(Wdu)], axis=1)
    gen = gen.reshape(128, 8, 4, 2, 2, 4, KH, 32).transpose(1, 3, 5, 7, 6, 4, 2, 0).reshape(NCHUNK, 128, CHUNK)

    arrays = {
        "x_tok": x, "x_feat": x.transpose(0, 2, 1), "cols_in": cols, "hbd_in": hbd.reshape(128, KH, 32),
        "ident_in": np.eye(128, dtype=np.float32), "base_in": base, "small_w": small, "wc_in": by_tile(Wc.T),
        "wqkv_in": by_tile(Wqkv.T), "wf1_in": by_tile(Wf1.T).reshape(128, -1), "wdelta_in": gen,
        "wf2_in": by_tile(Wf2.T).reshape(128, -1), "wo_in": by_tile(Wo.T).reshape(128, -1),
        "rows_in": np.broadcast_to(np.stack([bu, bo, bf2]), (128, 3, D)),
        "bcrow_in": np.broadcast_to(bc[4 * D:], (B, 2 * D)),
    }
    arrays = {k: np.ascontiguousarray(v) for k, v in arrays.items()}
    nc = bacc.Bacc("TRN2", target_bir_lowering=False, num_devices=1)
    args = {k: nc.dram_tensor(k, v.shape, mybir.dt.from_np(v.dtype), kind="ExternalInput").ap()
            for k, v in arrays.items()}
    args["out"] = nc.dram_tensor("out", (B, P, D), FP32, kind="ExternalOutput").ap()
    build(nc, **args)
    r = run(nc, [arrays], core_ids=[0])
    return r.results[0]["out"]
```
